# Optimizing a Trainium2 kernel written in Bass

```python
import numpy as np
import jax
import jax.numpy as jnp

def _softmax(x, axis=-1):
    return jax.nn.softmax(x, axis=axis)

def _gelu(x):
    return jax.nn.gelu(x, approximate=True)

def _silu(x):
    return jax.nn.silu(x)

def _sigmoid(x):
    return jax.nn.sigmoid(x)

def _layernorm(x, axis=-1, eps=1e-05):
    m = jnp.mean(x, axis=axis, keepdims=True)
    v = jnp.var(x, axis=axis, keepdims=True)
    return (x - m) / jnp.sqrt(v + eps)

def _scatter_add(tgt, idx, src, axis=0):
    return tgt.at[idx].add(src)

def _segment_sum(src, seg, n):
    return jax.ops.segment_sum(src, seg, n)
kernel_name = 'mk_perceiver_d2_seqx_r4_f507ff'

def setup_inputs(seed: int=0):
    np.random.seed(seed)
    _w = jnp.asarray

    def _rec_inputs():
        import jax
        import jax.numpy as jnp
        _rk = jax.random.key(seed)
        x = -0.0003929 + 0.9999 * jax.random.normal(jax.random.fold_in(_rk, 1), (1, 128, 256), jnp.float32)
        _lenS = 128 - jax.random.randint(jax.random.fold_in(_rk, 7), (1,), 0, max(1, 128 // 4) + 1, jnp.int32)
        _lenS2 = 12544 - jax.random.randint(jax.random.fold_in(_rk, 8), (1,), 0, max(1, 12544 // 4) + 1, jnp.int32)
        _ctx_768P = jax.random.normal(jax.random.fold_in(_rk, 11), (1, 16, 192), jnp.float32)
        _ctx_768c = jax.random.dirichlet(jax.random.fold_in(_rk, 511), 0.3 * jnp.ones((16,), jnp.float32), (1, 12544))
        _ctx_768t = jnp.einsum('bsk,bkd->bsd', _ctx_768c, _ctx_768P)
        _ctx_768t = _ctx_768t * jax.lax.rsqrt(jnp.mean(jnp.square(_ctx_768t)) + 1e-12) * 0.953939
        ctx_768 = -0.00055796 + 0.999787 * (_ctx_768t + 0.3 * jax.random.normal(jax.random.fold_in(_rk, 611), (1, 12544, 192), jnp.float32))
        return (x, ctx_768)
    x, ctx_768 = _rec_inputs()

    def _L0_xattn_setup():
        import jax, jax.numpy as jnp
        import numpy as np
        IMAGE_DIM = 256
        TEXT_DIM = 192
        NUM_HEADS = 16
        HEAD_DIM = IMAGE_DIM // NUM_HEADS
        key = jax.random.key(seed)
        ks = jax.random.split(key, 14)
        B, N, M = (4, 1024, 128)
        s_img = 1.0 / np.sqrt(IMAGE_DIM)
        s_txt = 1.0 / np.sqrt(TEXT_DIM)
        s_ff = 1.0 / np.sqrt(2 * IMAGE_DIM)
        return {'x': jax.random.normal(ks[0], (B, N, IMAGE_DIM), jnp.float32), 'y': jax.random.normal(ks[1], (B, M, TEXT_DIM), jnp.float32), 'Wq': jax.random.normal(ks[2], (IMAGE_DIM, IMAGE_DIM), jnp.float32) * s_img, 'bq': jax.random.normal(ks[3], (IMAGE_DIM,), jnp.float32) * s_img, 'Wk': jax.random.normal(ks[4], (TEXT_DIM, IMAGE_DIM), jnp.float32) * s_txt, 'bk': jax.random.normal(ks[5], (IMAGE_DIM,), jnp.float32) * s_txt, 'Wv': jax.random.normal(ks[6], (TEXT_DIM, IMAGE_DIM), jnp.float32) * s_txt, 'bv': jax.random.normal(ks[7], (IMAGE_DIM,), jnp.float32) * s_txt, 'W1': jax.random.normal(ks[8], (IMAGE_DIM, 2 * IMAGE_DIM), jnp.float32) * s_img, 'b1': jax.random.normal(ks[9], (2 * IMAGE_DIM,), jnp.float32) * s_img, 'W2': jax.random.normal(ks[10], (2 * IMAGE_DIM, IMAGE_DIM), jnp.float32) * s_ff, 'b2': jax.random.normal(ks[11], (IMAGE_DIM,), jnp.float32) * s_ff}
    _L0_xattn_all = _L0_xattn_setup()
    _L0_xattn_in = {k: v for k, v in _L0_xattn_all.items() if k in ('Wq', 'bq', 'Wk', 'bk', 'Wv', 'bv', 'W1', 'b1', 'W2', 'b2')}
    del _L0_xattn_all

    def _L0_attn_setup():
        import jax, jax.numpy as jnp
        import numpy as np
        B, S, NX, NH = (2, 512, 256, 16)
        HD = NX // NH
        key = jax.random.key(seed)
        k1, k2, k3 = jax.random.split(key, 3)
        return {'x': jax.random.normal(k1, (B, S, NX), dtype=jnp.float32), 'c_attn_w': jax.random.normal(k2, (NX, 3 * NX), dtype=jnp.float32) * 0.02, 'c_attn_b': jnp.zeros((3 * NX,), dtype=jnp.float32), 'c_proj_w': jax.random.normal(k3, (NX, NX), dtype=jnp.float32) * 0.02, 'c_proj_b': jnp.zeros((NX,), dtype=jnp.float32)}
    _L0_attn_all = _L0_attn_setup()
    _L0_attn_in = {k: v for k, v in _L0_attn_all.items() if k in ('c_attn_w', 'c_attn_b', 'c_proj_w', 'c_proj_b')}
    del _L0_attn_all

    def _L0_ffn_setup():
        import jax, jax.numpy as jnp
        import numpy as np
        B, S, D = (4, 512, 256)
        E = 8
        F = D * 4
        key = jax.random.key(seed)
        ks = jax.random.split(key, 8)
        sc = 0.02
        x = jax.random.normal(ks[0], (B, S, D), dtype=jnp.float32)
        Wg = jax.random.normal(ks[1], (D, E), dtype=jnp.float32) * sc
        bg = jnp.zeros((E,), dtype=jnp.float32)
        W1 = jax.random.normal(ks[2], (E, D, F), dtype=jnp.float32) * sc
        b1 = jnp.zeros((E, F), dtype=jnp.float32)
        W2 = jax.random.normal(ks[3], (E, F, D), dtype=jnp.float32) * sc
        b2 = jnp.zeros((E, D), dtype=jnp.float32)
        return {'x': x, 'Wg': Wg, 'bg': bg, 'W1': W1, 'b1': b1, 'W2': W2, 'b2': b2}
    _L0_ffn_all = _L0_ffn_setup()
    _L0_ffn_in = {k: v for k, v in _L0_ffn_all.items() if k in ('Wg', 'bg', 'W1', 'b1', 'W2', 'b2')}
    del _L0_ffn_all

    def _L1_xattn_setup():
        import jax, jax.numpy as jnp
        import numpy as np
        HEADS = 16
        DIM_HEAD = 64
        SCALE = DIM_HEAD ** (-0.5)
        QUERY_DIM = 256
        CONTEXT_DIM = 192
        INNER_DIM = HEADS * DIM_HEAD
        key = jax.random.key(seed)
        ks = jax.random.split(key, 7)
        B, Nq, Nk = (8, 1024, 77)
        x = jax.random.normal(ks[0], (B, Nq, QUERY_DIM), dtype=jnp.float32)
        context = jax.random.normal(ks[1], (B, Nk, CONTEXT_DIM), dtype=jnp.float32)
        Wq = jax.random.normal(ks[2], (QUERY_DIM, INNER_DIM), dtype=jnp.float32) * QUERY_DIM ** (-0.5)
        Wk = jax.random.normal(ks[3], (CONTEXT_DIM, INNER_DIM), dtype=jnp.float32) * CONTEXT_DIM ** (-0.5)
        Wv = jax.random.normal(ks[4], (CONTEXT_DIM, INNER_DIM), dtype=jnp.float32) * CONTEXT_DIM ** (-0.5)
        Wo = jax.random.normal(ks[5], (INNER_DIM, QUERY_DIM), dtype=jnp.float32) * INNER_DIM ** (-0.5)
        bo = jnp.zeros((QUERY_DIM,), dtype=jnp.float32)
        return {'x': x, 'context': context, 'Wq': Wq, 'Wk': Wk, 'Wv': Wv, 'Wo': Wo, 'bo': bo}
    _L1_xattn_all = _L1_xattn_setup()
    _L1_xattn_in = {k: v for k, v in _L1_xattn_all.items() if k in ('Wq', 'Wk', 'Wv', 'Wo', 'bo')}
    del _L1_xattn_all

    def _L1_attn_setup():
        import jax, jax.numpy as jnp
        import numpy as np
        D_MODEL = 256
        THRESH = 0.01
        key = jax.random.key(seed)
        kx, kw = jax.random.split(key)
        x = jax.random.normal(kx, (4, 512, D_MODEL), dtype=jnp.float32)
        W = jax.random.normal(kw, (D_MODEL, D_MODEL), dtype=jnp.float32) / np.sqrt(D_MODEL)
        return {'x': x, 'W': W}
    _L1_attn_all = _L1_attn_setup()
    _L1_attn_in = {k: v for k, v in _L1_attn_all.items() if k in ('W',)}
    del _L1_attn_all

    def _L1_ffn_setup():
        import jax, jax.numpy as jnp
        import numpy as np
        TOP_K = 2
        key = jax.random.key(seed)
        k1, k2, k3, k4, k5 = jax.random.split(key, 5)
        B, S, D, F, E = (2, 256, 256, 512, 8)
        return {'x': jax.random.normal(k1, (B, S, D), dtype=jnp.float32), 'router_kernel_DE': jax.random.normal(k2, (D, E), dtype=jnp.float32) * 0.02, 'kernel_gating_EDF': jax.random.normal(k3, (E, D, F), dtype=jnp.float32) * 0.02, 'kernel_up_EDF': jax.random.normal(k4, (E, D, F), dtype=jnp.float32) * 0.02, 'kernel_down_EFD': jax.random.normal(k5, (E, F, D), dtype=jnp.float32) * 0.02}
    _L1_ffn_all = _L1_ffn_setup()
    _L1_ffn_in = {k: v for k, v in _L1_ffn_all.items() if k in ('router_kernel_DE', 'kernel_gating_EDF', 'kernel_up_EDF', 'kernel_down_EFD')}
    del _L1_ffn_all
    return {'x': x, 'ctx_768': ctx_768, 'L0_xattn_Wq': _L0_xattn_in['Wq'], 'L0_xattn_bq': _L0_xattn_in['bq'], 'L0_xattn_Wk': _L0_xattn_in['Wk'], 'L0_xattn_bk': _L0_xattn_in['bk'], 'L0_xattn_Wv': _L0_xattn_in['Wv'], 'L0_xattn_bv': _L0_xattn_in['bv'], 'L0_xattn_W1': _L0_xattn_in['W1'], 'L0_xattn_b1': _L0_xattn_in['b1'], 'L0_xattn_W2': _L0_xattn_in['W2'], 'L0_xattn_b2': _L0_xattn_in['b2'], 'L0_attn_c_attn_w': _L0_attn_in['c_attn_w'], 'L0_attn_c_attn_b': _L0_attn_in['c_attn_b'], 'L0_attn_c_proj_w': _L0_attn_in['c_proj_w'], 'L0_attn_c_proj_b': _L0_attn_in['c_proj_b'], 'L0_ffn_Wg': _L0_ffn_in['Wg'], 'L0_ffn_bg': _L0_ffn_in['bg'], 'L0_ffn_W1': _L0_ffn_in['W1'], 'L0_ffn_b1': _L0_ffn_in['b1'], 'L0_ffn_W2': _L0_ffn_in['W2'], 'L0_ffn_b2': _L0_ffn_in['b2'], 'L1_xattn_Wq': _L1_xattn_in['Wq'], 'L1_xattn_Wk': _L1_xattn_in['Wk'], 'L1_xattn_Wv': _L1_xattn_in['Wv'], 'L1_xattn_Wo': _L1_xattn_in['Wo'], 'L1_xattn_bo': _L1_xattn_in['bo'], 'L1_attn_W': _L1_attn_in['W'], 'L1_ffn_router_kernel_DE': _L1_ffn_in['router_kernel_DE'], 'L1_ffn_kernel_gating_EDF': _L1_ffn_in['kernel_gating_EDF'], 'L1_ffn_kernel_up_EDF': _L1_ffn_in['kernel_up_EDF'], 'L1_ffn_kernel_down_EFD': _L1_ffn_in['kernel_down_EFD']}

def reference(x, ctx_768, L0_xattn_Wq, L0_xattn_bq, L0_xattn_Wk, L0_xattn_bk, L0_xattn_Wv, L0_xattn_bv, L0_xattn_W1, L0_xattn_b1, L0_xattn_W2, L0_xattn_b2, L0_attn_c_attn_w, L0_attn_c_attn_b, L0_attn_c_proj_w, L0_attn_c_proj_b, L0_ffn_Wg, L0_ffn_bg, L0_ffn_W1, L0_ffn_b1, L0_ffn_W2, L0_ffn_b2, L1_xattn_Wq, L1_xattn_Wk, L1_xattn_Wv, L1_xattn_Wo, L1_xattn_bo, L1_attn_W, L1_ffn_router_kernel_DE, L1_ffn_kernel_gating_EDF, L1_ffn_kernel_up_EDF, L1_ffn_kernel_down_EFD):
    import jax
    import jax.numpy as jnp

    def _L0_xattn_ref(x, y, Wq, bq, Wk, bk, Wv, bv, W1, b1, W2, b2):
        import jax, jax.numpy as jnp
        import numpy as np
        IMAGE_DIM = 256
        TEXT_DIM = 192
        NUM_HEADS = 16
        HEAD_DIM = IMAGE_DIM // NUM_HEADS
        B, N, _ = x.shape
        M = y.shape[1]
        q = (x @ Wq + bq).reshape(B, N, NUM_HEADS, HEAD_DIM)
        k = (y @ Wk + bk).reshape(B, M, NUM_HEADS, HEAD_DIM)
        v = (y @ Wv + bv).reshape(B, M, NUM_HEADS, HEAD_DIM)
        scale = 1.0 / np.sqrt(HEAD_DIM)
        scores = jnp.einsum('bnhd,bmhd->bhnm', q, k) * scale
        attn = jax.nn.softmax(scores, axis=-1)
        out = jnp.einsum('bhnm,bmhd->bnhd', attn, v).reshape(B, N, IMAGE_DIM)
        h = jax.nn.relu(out @ W1 + b1)
        return h @ W2 + b2

    def _L0_attn_ref(x, c_attn_w, c_attn_b, c_proj_w, c_proj_b):
        import jax, jax.numpy as jnp
        import numpy as np
        B, S, NX, NH = (2, 512, 256, 16)
        HD = NX // NH
        b, s, nx = x.shape
        qkv = x @ c_attn_w + c_attn_b
        q, k, v = jnp.split(qkv, 3, axis=-1)
        q = q.reshape(b, s, NH, HD).transpose(0, 2, 1, 3)
        k = k.reshape(b, s, NH, HD).transpose(0, 2, 1, 3)
        v = v.reshape(b, s, NH, HD).transpose(0, 2, 1, 3)
        w = jnp.einsum('bhqd,bhkd->bhqk', q, k) / jnp.sqrt(jnp.float32(HD))
        causal = jnp.tril(jnp.ones((s, s), dtype=bool))
        w = jnp.where(causal[None, None, :, :], w, jnp.float32(-10000000000.0))
        w = jax.nn.softmax(w, axis=-1)
        a = jnp.einsum('bhqk,bhkd->bhqd', w, v)
        a = a.transpose(0, 2, 1, 3).reshape(b, s, nx)
        return a @ c_proj_w + c_proj_b

    def _L0_ffn_ref(x, Wg, bg, W1, b1, W2, b2):
        import jax, jax.numpy as jnp
        import numpy as np
        B, S, D = (4, 512, 256)
        E = 8
        F = D * 4
        batch, seq, dim = x.shape
        flat_x = x.reshape(-1, dim)
        logits = flat_x @ Wg + bg
        probs = jax.nn.softmax(logits, axis=-1)
        top_w, top_i = jax.lax.top_k(probs, 2)
        top_w = top_w / (jnp.sum(top_w, axis=-1, keepdims=True) + 1e-06)
        out = jnp.zeros_like(flat_x)
        n_experts = W1.shape[0]
        for e in range(n_experts):
            w_e = jnp.sum(top_w * (top_i == e).astype(top_w.dtype), axis=-1)
            h = jax.nn.gelu(flat_x @ W1[e] + b1[e], approximate=True)
            eo = h @ W2[e] + b2[e]
            out = out + eo * w_e[:, None]
        return out.reshape(batch, seq, dim)

    def _L1_xattn_ref(x, context, Wq, Wk, Wv, Wo, bo):
        import jax, jax.numpy as jnp
        import numpy as np
        HEADS = 16
        DIM_HEAD = 64
        SCALE = DIM_HEAD ** (-0.5)
        QUERY_DIM = 256
        CONTEXT_DIM = 192
        INNER_DIM = HEADS * DIM_HEAD
        B, Nq, _ = x.shape
        Nk = context.shape[1]
        q = x @ Wq
        k = context @ Wk
        v = context @ Wv
        q = q.reshape(B, Nq, HEADS, DIM_HEAD).transpose(0, 2, 1, 3)
        k = k.reshape(B, Nk, HEADS, DIM_HEAD).transpose(0, 2, 1, 3)
        v = v.reshape(B, Nk, HEADS, DIM_HEAD).transpose(0, 2, 1, 3)
        sim = jnp.einsum('bhid,bhjd->bhij', q, k) * SCALE
        attn = jax.nn.softmax(sim, axis=-1)
        out = jnp.einsum('bhij,bhjd->bhid', attn, v)
        out = out.transpose(0, 2, 1, 3).reshape(B, Nq, INNER_DIM)
        return out @ Wo + bo

    def _L1_attn_ref(x, W):
        import jax, jax.numpy as jnp
        import numpy as np
        D_MODEL = 256
        THRESH = 0.01
        B, T, D = x.shape
        scale = 1.0 / jnp.sqrt(jnp.asarray(D, x.dtype))
        scores = jnp.einsum('btd,bsd->bts', x, x) * scale
        probs = jax.nn.softmax(scores, axis=-1)
        vacuum_mask = probs < THRESH
        vacuum_energy = jnp.where(vacuum_mask, probs, 0.0)
        vac_sum = vacuum_energy.sum(axis=-1, keepdims=True)
        vac_in = jnp.broadcast_to(vac_sum, (B, T, D))
        casimir = jnp.einsum('btd,od->bto', vac_in, W)
        sparse_probs = jnp.where(vacuum_mask, 0.0, probs)
        sparse_probs = sparse_probs / (sparse_probs.sum(axis=-1, keepdims=True) + 1e-09)
        attended = jnp.einsum('bts,bsd->btd', sparse_probs, x)
        return attended + casimir * 0.01

    def _L1_ffn_ref(x, router_kernel_DE, kernel_gating_EDF, kernel_up_EDF, kernel_down_EFD):
        import jax, jax.numpy as jnp
        import numpy as np
        TOP_K = 2
        E = router_kernel_DE.shape[-1]
        x = x.astype(jnp.float32)
        logits_BSE = jnp.einsum('BSD,DE->BSE', x, router_kernel_DE)
        probs_BSE = jax.nn.softmax(logits_BSE.astype(jnp.float32), axis=-1)
        weights_BSK, indices_BSK = jax.lax.top_k(probs_BSE, TOP_K)
        norm_weights_BSK = jax.nn.softmax(weights_BSK, axis=-1)
        one_hot_BSKE = jax.nn.one_hot(indices_BSK, num_classes=E, dtype=x.dtype)
        full_weights_BSE = jnp.sum(one_hot_BSKE * norm_weights_BSK[..., None], axis=2)
        gating_BSEF = jnp.einsum('BSD,EDF->BSEF', x, kernel_gating_EDF)
        act_BSEF = jax.nn.silu(gating_BSEF)
        up_BSEF = jnp.einsum('BSD,EDF->BSEF', x, kernel_up_EDF)
        fuse_BSEF = act_BSEF * up_BSEF
        down_BSED = jnp.einsum('BSEF,EFD->BSED', fuse_BSEF, kernel_down_EFD)
        out_BSD = jnp.einsum('BSED,BSE->BSD', down_BSED, full_weights_BSE)
        return out_BSD.astype(jnp.float32)
    x = x + _L0_xattn_ref(_layernorm(x, axis=-1), ctx_768, L0_xattn_Wq, L0_xattn_bq, L0_xattn_Wk, L0_xattn_bk, L0_xattn_Wv, L0_xattn_bv, L0_xattn_W1, L0_xattn_b1, L0_xattn_W2, L0_xattn_b2)
    x = x + _L0_attn_ref(_layernorm(x, axis=-1), L0_attn_c_attn_w, L0_attn_c_attn_b, L0_attn_c_proj_w, L0_attn_c_proj_b)
    x = x + _L0_ffn_ref(_layernorm(x, axis=-1), L0_ffn_Wg, L0_ffn_bg, L0_ffn_W1, L0_ffn_b1, L0_ffn_W2, L0_ffn_b2)
    x = x + _L1_xattn_ref(_layernorm(x, axis=-1), ctx_768, L1_xattn_Wq, L1_xattn_Wk, L1_xattn_Wv, L1_xattn_Wo, L1_xattn_bo)
    x = x + _L1_attn_ref(_layernorm(x, axis=-1), L1_attn_W)
    x = x + _L1_ffn_ref(_layernorm(x, axis=-1), L1_ffn_router_kernel_DE, L1_ffn_kernel_gating_EDF, L1_ffn_kernel_up_EDF, L1_ffn_kernel_down_EFD)
    return x

_drawn_inputs = setup_inputs


def setup_inputs(seed=0):
    import zlib

    import numpy as np

    out = dict(_drawn_inputs(seed))
    spreads = {'L0_attn_c_attn_b': (0.0, 0.1),
     'L0_attn_c_proj_b': (0.0, 0.1),
     'L0_ffn_bg': (0.0, 0.1),
     'L0_ffn_b1': (0.0, 0.362),
     'L0_ffn_b2': (0.0, 0.1),
     'L1_xattn_bo': (0.0, 0.1)}
    factors = {'L0_xattn_bq': 5.122,
     'L0_xattn_bk': 8.0,
     'L1_attn_W': 8.0,
     'L1_ffn_router_kernel_DE': 8.0,
     'L1_ffn_kernel_gating_EDF': 7.504,
     'L1_ffn_kernel_up_EDF': 7.4,
     'L1_ffn_kernel_down_EFD': 7.369}
    for name, (base, spread) in spreads.items():
        noise = np.random.default_rng([zlib.crc32(name.encode()), seed]).standard_normal(out[name].shape)
        drawn = base * np.exp(spread * noise) if base else spread * noise
        out[name] = jnp.asarray(drawn.astype(out[name].dtype))
    for name, factor in factors.items():
        out[name] = (out[name] * factor).astype(out[name].dtype)
    return out
```

```python
from contextlib import ExitStack

import concourse.bass as bass
from concourse import mybir

F32 = mybir.dt.float32
F16 = mybir.dt.float16
ALU = mybir.AluOpType
ACT = mybir.ActivationFunctionType
AX = mybir.AxisListType

P = 128
EPS = 1e-5
EXP_SHIFT = 8 * 0.6931471805599453


class Queue:

    def __init__(self, sem):
        self.sem, self.count, self.steps, self.known = sem, 0, [], {}

    def do(self, build):
        self.steps.append([build, None])
        return self

    def mark(self):
        assert self.steps[-1][1] is None
        self.count += 1
        self.steps[-1][1] = self.sem
        return (self.sem, self.count)

    def wait(self, *tokens):
        for sem, value in tokens:
            if self.known.get(sem.name, 0) < value:
                self.known[sem.name] = value
                self.steps.append([lambda e, s=sem, v=value: e.wait_ge(s, v), "wait"])
        return self

    def settle(self):
        token = self.mark()
        self.wait(token)
        return token

    def run(self, engine):
        for build, sem in self.steps:
            ins = build(engine)
            if sem is not None and sem != "wait":
                ins.then_inc(sem, 1)


class Landing:

    def __init__(self, sem):
        self.sem, self.total = sem, 0

    def load(self, queue, out, in_):
        self.total += 16
        queue.steps.append([lambda e, o=out, i=in_, s=self.sem: e.dma_start(o, i).then_inc(s, 16), "wait"])
        return (self.sem, self.total)


def perceiver_kernel(nc, d, out):
    _, N_TOK, D = d["x"].shape
    _, M, C = d["ctx_768"].shape
    H = 16
    NE = d["L0_ffn_Wg"].shape[1]
    F0 = d["L0_ffn_W1"].shape[2]
    F1 = d["L1_ffn_kernel_gating_EDF"].shape[2]
    assert N_TOK == P and D == 2 * P and C == 192 and M % P == 0
    NT = M // P
    CH = 7
    NCH = NT // CH
    assert NT % CH == 0
    CW = CH * C
    NW = 2 * C + 2
    ONE = C
    LO = C + 2
    MAXC = 448
    MAXB = 4
    NMAX = M // (MAXC * MAXB)
    assert NMAX * MAXC * MAXB == M
    CB_ROW = C - P
    R_ROW, C_ROW, K_C = 64, 66, 68

    ctx = ExitStack()
    with ctx:
        def sb(name, shape, dt):
            return ctx.enter_context(nc.sbuf_tensor(name, shape, dt))

        def sem(name):
            return ctx.enter_context(nc.semaphore(name))

        ctxT_a_hi = sb("ctxT_a_hi", [P, M], F16)
        ctxT_a_lo = sb("ctxT_a_lo", [P, M], F16)
        ctxT_b = sb("ctxT_b", [P, M], F16)
        ctxT_c = sb("ctxT_c", [P, M], F16)
        q_all = sb("q_all", [P, 5, H * P], F16)
        q_a_hi, q_a_lo, q_b, q_c, q_m = (q_all[:, n, :] for n in range(5))
        scratch = q_all[:, :, :].rearrange("p a b -> p (a b)").bitcast(F32)
        p16 = sb("p16", [P, 4, 8 * P], F16)
        ctx32 = sb("ctx32", [P, 2, CW], F32)
        ctx16 = sb("ctx16", [P, 2, CH, NW], F16)
        W = sb("W", [P, 10240], F32)
        x = sb("x_tok", [P, D], F32)
        xn = sb("xn", [P, D], F32)
        xnT = sb("xnT", [P, 2, P], F32)
        att = sb("att", [P, 1024], F32)
        U = sb("U", [P, 4, C], F32)
        uT_a = sb("uT_a", [P, 4 * P], F32)
        uT_b = sb("uT_b", [CB_ROW, 4 * P], F32)
        ident = sb("ident", [P, P], F32)
        ident16 = sb("ident16", [P, P], F16)
        causal = sb("causal", [P, P], F32)
        head16 = sb("head16", [P, 8], F32)
        head64 = sb("head64", [P, 2], F32)
        lower = sb("lower", [P, NE, NE], F32)
        bias_rows = sb("bias_rows", [8, D], F32)
        col_in = sb("col_in", [P, P], F32)
        cols = sb("cols", [P, P], F32)
        small = sb("small", [P, 512], F32)
        minus_half = sb("minus_half", [P, 1], F32)
        ps = ctx.enter_context(nc.psum_tensor("ps", [P, 8, 512], F32))

        def row_select(n):
            return ident[0:8, n:n + 1].to_broadcast([8, P])

        pe, act, dve, pool, sp = (Queue(sem(f"{n}_done")) for n in ("pe", "act", "dve", "pool", "sp"))
        ld_x = Landing(sem("ld_x"))
        ld_bias = Landing(sem("ld_bias"))
        ld_w = Landing(sem("ld_w"))
        ld_w2 = Landing(sem("ld_w2"))
        ld_exp = [Landing(sem(f"ld_exp{n}")) for n in range(2)]
        ld_ctx = [Landing(sem(f"ld_ctx{n}")) for n in range(2)]
        ld_rows = Landing(sem("ld_rows"))
        st_out = Landing(sem("st_out"))

        def mm(out, lhsT, rhs, start, stop, **kw):
            pe.do(lambda e: e.matmul(out, lhsT, rhs, start=start, stop=stop, **kw))

        def tp(out, in_, idt):
            pe.do(lambda e: e.transpose(out, in_, idt))

        def copy(q, out, in_):
            if q is act:
                q.do(lambda e: e.copy(out, in_))
            else:
                q.do(lambda e: e.tensor_copy(out, in_))

        def tt(q, out, a, b, op):
            q.do(lambda e: e.tensor_tensor(out, a, b, op))

        def ts(q, out, a, s1, s2, op0, op1=None):
            if op1 is None:
                q.do(lambda e: e.tensor_scalar(out, a, s1, None, op0))
            else:
                q.do(lambda e: e.tensor_scalar(out, a, s1, s2, op0, op1))

        def reduce(out, in_, axis, op):
            return dve.do(lambda e: e.tensor_reduce(out, in_, axis, op))

        def reciprocal(out, in_):
            return dve.do(lambda e: e.reciprocal(out, in_))

        def exp(out, in_, scale=1.0):
            act.do(lambda e: e.activation(out, in_, ACT.Exp, scale=scale))

        def gelu(out, in_, bias):
            act.do(lambda e: e.activation(out, in_, ACT.Gelu_apprx_tanh, bias=bias))

        def weigh(y, w):
            dve.do(lambda e: e.scalar_tensor_tensor(out=x[:, :], in0=y, scalar=w, in1=x[:, :],
                                                    op0=ALU.mult, op1=ALU.add))

        def bc(ap, axis, shape):
            return ap.unsqueeze(axis).to_broadcast(shape)

        def layernorm(ready):
            stats, mv, rstd = small[:, 0:6], small[:, 6:8], small[:, 8:9]
            dve.wait(*ready)
            dve.do(lambda e: e.bn_stats(stats, x[:, :])).settle()
            dve.do(lambda e: e.bn_aggr(mv, stats)).settle()
            ts(dve, rstd, mv[:, 1:2], EPS, None, ALU.add)
            var_ready = dve.mark()
            pool.wait(var_ready)
            tt(pool, rstd, rstd, minus_half[:, :], ALU.pow)
            rstd_ready = pool.mark()
            dve.wait(rstd_ready)
            ts(dve, xn[:, :], x[:, :], mv[:, 0:1], rstd, ALU.subtract, ALU.mult)
            normed = dve.mark()
            pe.wait(normed)
            for i in range(2):
                tp(ps[:, 0, i * P:(i + 1) * P], xn[:, i * P:(i + 1) * P], ident[:, :])
            turned = pe.mark()
            act.wait(turned)
            copy(act, xnT[:, :, :], ps[:, 0, 0:2 * P].rearrange("p (a b) -> p a b", a=2))
            return act.mark()

        def residual(y, ready):
            dve.wait(ready)
            tt(dve, x[:, :], y, x[:, :], ALU.add)
            return dve.settle()

        def transpose_act(src, n, dst, ready, bank, idt=None):
            pe.wait(*ready)
            for i in range(n):
                tp(ps[:, bank + i // 4, (i % 4) * P:(i % 4 + 1) * P], src[:, i * P:(i + 1) * P], ident[:, :])
            turned = pe.mark()
            act.wait(turned)
            nb = -(-n // 4)
            w = min(n, 4) * P
            copy(act, dst.rearrange("p (b i) q -> p b (i q)", b=nb), ps[:, bank:bank + nb, 0:w])
            return act.mark()

        pool.do(lambda e: e.memset(ident[:, :], 0.0))
        pool.do(lambda e: e.memset(causal[:, :], 0.0))
        pool.do(lambda e: e.memset(minus_half[:, :], -0.5))
        pool.do(lambda e: e.memset(head16[:, :], 1.0))
        pool.do(lambda e: e.memset(head64[:, :], 1.0))
        pool.do(lambda e: e.memset(lower[:, :, :], 1.0)).settle()
        pool.do(lambda e: e.affine_select(out=ident[:, :], in_=ident[:, :], compare_op=ALU.not_equal,
                                          fill=1.0, base=0, pattern=[[-1, P]], channel_multiplier=1))
        pool.do(lambda e: e.affine_select(out=causal[:, :], in_=causal[:, :], compare_op=ALU.is_ge,
                                          fill=-1e10, base=0, pattern=[[-1, P]], channel_multiplier=1))
        for t, n, w in ((head16, 8, 16), (head64, 2, 64)):
            pool.do(lambda e, t=t, n=n, w=w: e.affine_select(
                out=t[:, :], in_=t[:, :], compare_op=ALU.is_ge, fill=0.0, base=0,
                pattern=[[-w, n]], channel_multiplier=1))
        pool.settle()
        for t, n, w in ((head16, 8, 16), (head64, 2, 64)):
            pool.do(lambda e, t=t, n=n, w=w: e.affine_select(
                out=t[:, :], in_=t[:, :], compare_op=ALU.is_ge, fill=0.0, base=w - 1,
                pattern=[[w, n]], channel_multiplier=-1))
        pool.do(lambda e: e.affine_select(out=lower[:, :, :], in_=lower[:, :, :], compare_op=ALU.is_ge,
                                          fill=0.0, base=-1, pattern=[[1, NE], [-1, NE]],
                                          channel_multiplier=0))
        constants = pool.mark()
        for n in range(2):
            dve.do(lambda e, n=n: e.memset(ctx16[:, n, :, ONE:ONE + 1], 1.0))
            dve.do(lambda e, n=n: e.memset(ctx16[:, n, :, ONE + 1:LO], 0.0))
        dve.do(lambda e: e.memset(ctxT_c[CB_ROW:P, :], 1.0))
        dve.do(lambda e: e.memset(q_c[CB_ROW:P, :], 0.0))
        dve.do(lambda e: e.memset(q_m[CB_ROW:P, :], 0.0))
        dve.do(lambda e: e.memset(bias_rows[:, :], 0.0))
        dve.do(lambda e: e.memset(col_in[:, :], 0.0))
        blank = dve.mark()
        dve.wait(constants)
        copy(dve, ident16[:, :], ident[:, :])
        ident16_ready = dve.mark()

        x_in = ld_x.load(sp, x[:, :], d["x"][0])
        sp.wait(blank)
        BR = {}
        for n, (name, lo_, w) in enumerate((("L0_xattn_b2", 0, D), ("L0_attn_c_attn_b", 2 * D, D),
                                            ("L0_attn_c_proj_b", 0, D), ("L1_xattn_bo", 0, D),
                                            ("L0_ffn_bg", 0, NE))):
            BR[name] = n
            biases_in = ld_bias.load(sp, bias_rows[n:n + 1, 0:w],
                                     d[name].rearrange("(a n) -> a n", a=1)[:, lo_:lo_ + w])
        CL, row = {}, 0
        for name, n in (("L0_xattn_bq", 2), ("L0_xattn_bk", 2), ("L0_xattn_bv", 2), ("L0_xattn_b1", 4),
                        ("L0_attn_c_attn_b", 4)):
            CL[name] = row
            biases_in = ld_bias.load(sp, col_in[row:row + n, :],
                                     d[name].rearrange("(r n) -> r n", n=P)[0:n, :])
            row += n
        CL["L0_ffn_b1"] = row
        nb1 = NE * F0 // P
        biases_in = ld_bias.load(sp, col_in[row:row + nb1, :],
                                 d["L0_ffn_b1"].rearrange("e (r n) -> (e r) n", n=P))

        def col(name, i):
            return cols[:, CL[name] + i:CL[name] + i + 1]

        pe.wait(constants, biases_in)
        tp(ps[:, 1, 0:P], col_in[:, :], ident[:, :])
        turned = pe.mark()
        act.wait(turned)
        copy(act, cols[:, :], ps[:, 1, 0:P])
        cols_ready = act.mark()

        def wview(off, a, b):
            return W[:, off:off + a * b].rearrange("p (a b) -> p a b", a=a)

        def load_split(landing, off, src, n):
            landing.load(sp, W[:, off:off + n], src[0:P, :])
            return landing.load(sp, W[0:CB_ROW, off + n:off + 2 * n], src[P:C, :])

        class XA:
            pass

        L0 = XA()
        L0.dh, L0.hp, L0.mask, L0.scale = 16, 8, head16, 0.25
        L0.wq, L0.wk, L0.wkT, L0.wv = 0, 512, 1024, 1536
        L0.inner = H * L0.dh
        L1 = XA()
        L1.dh, L1.hp, L1.mask, L1.scale = 64, 2, head64, 0.125
        L1.wq, L1.wk, L1.wkT, L1.wv, L1.wo = 0, 2048, 4096, 6144, 8192
        L1.inner = H * L1.dh
        W1_OFF, W2_OFF = 2048, 3072
        CA_OFF, CP_OFF = 4096, 5632

        ld_w.load(sp, wview(L0.wq, 2, D), d["L0_xattn_Wq"].rearrange("(a p) n -> p a n", p=P))
        l0_proj_in = load_split(ld_w, L0.wk, d["L0_xattn_Wk"], L0.inner)

        ctx_dram = d["ctx_768"][0].rearrange("(p t) c -> p (t c)", p=P)
        chunk_count = [0]
        split_done = [None, None]
        read_done = [(), ()]

        def load_chunk(c):
            slot = chunk_count[0] % 2
            chunk_count[0] += 1
            if split_done[slot]:
                sp.wait(*split_done[slot])
            return slot, ld_ctx[slot].load(sp, ctx32[:, slot, :], ctx_dram[:, c * CW:(c + 1) * CW])

        def chunk32(slot):
            return ctx32[:, slot, :].rearrange("p (t c) -> p t c", t=CH)

        def build_ctxT(c):
            slot, landed = load_chunk(c)
            hi, lo = ctx16[:, slot, :, 0:C], ctx16[:, slot, :, LO:NW]
            act.wait(landed, blank, *read_done[slot])
            copy(act, hi, chunk32(slot))
            hi_ready = act.mark()
            dve.wait(landed, hi_ready, *read_done[slot])
            tt(dve, lo, chunk32(slot), hi, ALU.subtract)
            lo_ready = dve.mark()
            split_done[slot] = (lo_ready,)
            bank = 3 * (c % 2)
            b16 = ps[:, bank:bank + 3, :].rearrange("p a b -> p (a b)").bitcast(F16).rearrange("p (a b) -> p a b", a=3)
            pe.wait(lo_ready, ident16_ready, *evacuated[c % 2])
            for t in range(CH):
                s = slice(t * P, (t + 1) * P)
                tp(b16[:, 0, s], ctx16[:, slot, t, 0:P], ident16[:, :])
                tp(b16[0:CB_ROW, 1, s], ctx16[:, slot, t, P:C], ident16[:, :])
                tp(b16[CB_ROW:P, 1, s], ctx16[:, slot, t, LO + P:NW], ident16[:, :])
                tp(b16[:, 2, s], ctx16[:, slot, t, LO:LO + P], ident16[:, :])
            turned = pe.mark()
            read_done[slot] = (turned,)
            s = slice(c * CH * P, (c + 1) * CH * P)
            act.wait(turned)
            copy(act, ctxT_a_hi[:, s], b16[:, 0, 0:CH * P])
            copy(act, ctxT_b[:, s], b16[:, 1, 0:CH * P])
            e1 = act.mark()
            dve.wait(turned)
            copy(dve, ctxT_a_lo[:, s], b16[:, 2, 0:CH * P])
            e2 = dve.mark()
            pool.wait(e1)
            copy(pool, ctxT_c[0:CB_ROW, s], ctxT_b[0:CB_ROW, s])
            evacuated[c % 2] = (e1, e2)
            return (e1, e2, pool.mark())

        def xattn(L, wq_ready, bq, bk, xnT_ready, while_max=None):
            nI = L.inner // P
            hp = L.hp
            wq, wkT = wview(L.wq, 2, L.inner), wview(L.wkT, nI, 256)
            wkA, wkB = W[:, L.wk:L.wk + L.inner], W[0:CB_ROW, L.wk + L.inner:L.wk + 2 * L.inner]
            wvA, wvB = W[:, L.wv:L.wv + L.inner], W[0:CB_ROW, L.wv + L.inner:L.wv + 2 * L.inner]
            qT = p16[:, 0, 0:2 * P].bitcast(F32)
            spread = p16[:, 1:3, :].rearrange("p a b -> p (a b)").bitcast(F32)[:, 0:hp * P].rearrange(
                "p (h q) -> p h q", h=hp)
            pe.wait(wq_ready, constants)
            for i in range(0, nI, 2):
                bank = 2 + (i // 2) % 2
                if i >= 4:
                    pe.wait(wkT_evac[i // 2 - 2])
                for j in range(2):
                    tp(ps[:, bank, j * C:j * C + P], wkA[:, (i + j) * P:(i + j + 1) * P], ident[:, :])
                    tp(ps[:, bank, j * C + P:(j + 1) * C], wkB[:, (i + j) * P:(i + j + 1) * P],
                       ident[0:CB_ROW, 0:CB_ROW])
                turned = pe.mark()
                act.wait(turned)
                src = ps[:, bank, 0:2 * C].rearrange("p (j c) -> p j c", j=2)
                copy(act, wkT[:, i:i + 2, 0:C], src)
                copy(act, wkT[:, i:i + 2, C:256], src[:, :, P:C])
                if i == 0:
                    wkT_evac = []
                wkT_evac.append(act.mark())
            pe.wait(wkT_evac[-1], xnT_ready)
            folded, q_free, spread_free = [], (), None
            c16 = p16
            for i in range(nI):
                pe.wait(*q_free)
                for a in range(2):
                    mm(ps[:, 1, 0:P], wq[:, a, i * P:(i + 1) * P], xnT[:, a, :], a == 0, a == 1)
                q_ready = pe.mark()
                dve.wait(q_ready)
                if bq:
                    ts(dve, qT, ps[:, 1, 0:P], col(bq, i), L.scale, ALU.add, ALU.mult)
                else:
                    ts(dve, qT, ps[:, 1, 0:P], L.scale, None, ALU.mult)
                q_free = (dve.settle(),)
                if spread_free:
                    dve.wait(spread_free)
                tt(dve, spread, bc(qT, 1, [P, hp, P]), bc(L.mask[:, :], 2, [P, hp, P]), ALU.mult)
                spread_ready = dve.mark()
                for j in range(0, hp, 4):
                    nh = min(4, hp)
                    w = nh * P
                    n = len(folded)
                    bank = 2 + 3 * (n % 2)
                    pe.wait(spread_ready)
                    if n >= 2:
                        pe.wait(*folded[n - 2])
                    rhs = spread[:, j:j + nh, :]
                    mm(ps[:, bank, 0:w], wkT[:, i, 0:P], rhs, True, True)
                    mm(ps[:, bank + 1, 0:w], wkT[:, i, P:256], rhs, True, True)
                    if bk:
                        mm(ps[0:1, bank + 2, 0:w], col(bk, i), rhs, True, True)
                    got = pe.mark()
                    spread_free = got
                    s = slice((i * hp + j) * P, (i * hp + j + nh) * P)
                    act.wait(got)
                    copy(act, q_a_hi[:, s], ps[:, bank, 0:w])
                    copy(act, q_b[:, s], ps[:, bank + 1, 0:w])
                    hi_ready = act.mark()
                    dve.wait(hi_ready)
                    tt(dve, q_a_lo[:, s], ps[:, bank, 0:w], q_a_hi[:, s], ALU.subtract)
                    tt(dve, q_c[0:CB_ROW, s], ps[0:CB_ROW, bank + 1, 0:w], q_b[0:CB_ROW, s], ALU.subtract)
                    copy(dve, q_m[0:CB_ROW, s], q_b[0:CB_ROW, s])
                    if bk:
                        chi, clo = uT_a[0:1, :].bitcast(F16)[:, 0:512], uT_a[0:1, :].bitcast(F16)[:, 512:1024]
                        if n:
                            dve.wait(rows_in)
                        copy(dve, chi, ps[0:1, bank + 2, 0:w])
                        dve.settle()
                        tt(dve, clo, ps[0:1, bank + 2, 0:w], chi, ALU.subtract)
                    done = dve.mark()
                    folded.append((done,))
                    if bk:
                        sp.wait(done)
                        for q in (q_c, q_m):
                            for r, part in ((C_ROW, chi), (C_ROW + 1, clo)):
                                rows_in = ld_rows.load(sp, q[r:r + 1, s], part)
                        pe_rows = rows_in
            q_done = folded[-1]

            pe.wait(*q_done, *folded[-2])
            if bk:
                pe.wait(pe_rows)
            mpart = small[:, 64:64 + H * NMAX].rearrange("p (h s) -> p h s", h=H)
            mx = small[:, 192:192 + H]
            reduced = [None, None]
            for h in range(H):
                hs = slice(h * P, (h + 1) * P)
                for s in range(NMAX):
                    half = (h * NMAX + s) % 2
                    if reduced[half]:
                        pe.wait(reduced[half])
                    for b in range(MAXB):
                        k0 = (s * MAXB + b) * MAXC
                        if h == 0:
                            pe.wait(*ctxT_ready[-(-(k0 + MAXC) // (CH * P)) - 1])
                        o = ps[:, half * 4 + b, 0:MAXC]
                        mm(o, q_a_hi[:, hs], ctxT_a_hi[:, k0:k0 + MAXC], True, False)
                        mm(o, q_m[0:K_C, hs], ctxT_c[0:K_C, k0:k0 + MAXC], False, True)
                    scored = pe.mark()
                    dve.wait(scored)
                    reduce(
                        mpart[:, h, s:s + 1], ps[:, half * 4:half * 4 + 4, 0:MAXC], AX.XY, ALU.max)
                    reduced[half] = dve.mark()
            dve.wait(reduced[0], reduced[1])
            reduce(mx, mpart, AX.X, ALU.max).settle()
            ts(dve, mx, mx, -1.0, EXP_SHIFT, ALU.mult, ALU.add)
            shift_ready = dve.mark()
            pe.wait(shift_ready)
            for h in range(H):
                tp(ps[0:1, h // 4, (h % 4) * P:(h % 4 + 1) * P], mx[:, h:h + 1], ident[:, :])
            turned = pe.mark()
            rhi, rlo = (p16[0:1, n:n + 2, :].rearrange("p a b -> p (a b)") for n in (0, 2))
            row = ps[0:1, 0:4, :].rearrange("p a b -> p (a b)")
            dve.wait(turned)
            copy(dve, rhi, row)
            dve.settle()
            tt(dve, rlo, row, rhi, ALU.subtract)
            rows_ready = dve.mark()
            sp.wait(rows_ready)
            for n, part in enumerate((rhi, rlo)):
                rows_in = ld_rows.load(sp, q_c[R_ROW + n:R_ROW + n + 1, :], part)
            pe.wait(rows_in)

            sc_free = [None, None]
            p_free = [None, None]
            att_ready = ()
            for g in range(2):
                qs = slice(g * 8 * P, (g + 1) * 8 * P)
                pending = None
                for t in range(NT + 1):
                    if t < NT and t % CH == 0:
                        slot, landed = load_chunk(t // CH)
                        hi, lo = ctx16[:, slot, :, 0:C], ctx16[:, slot, :, LO:NW]
                        pool.wait(landed, *read_done[slot])
                        copy(pool, hi, chunk32(slot))
                        pool.settle()
                        tt(pool, lo, chunk32(slot), hi, ALU.subtract)
                        chunk_ready = pool.mark()
                        split_done[slot] = (chunk_ready,)
                    if t < NT:
                        b = t % 2
                        ks = slice(t * P, (t + 1) * P)
                        if sc_free[b]:
                            pe.wait(sc_free[b])
                        if t == 0:
                            pe.wait(*att_ready)
                        terms = ((ctxT_a_hi[:, ks], q_a_hi), (ctxT_a_hi[:, ks], q_a_lo),
                                 (ctxT_a_lo[:, ks], q_a_hi), (ctxT_b[:, ks], q_b),
                                 (ctxT_c[0:K_C, ks], q_c))
                        for n, (key, q) in enumerate(terms):
                            for j in range(2):
                                rhs = q[0:key.shape[0], g * 1024 + j * 512:g * 1024 + (j + 1) * 512]
                                mm(ps[:, 2 * b + j, :], key, rhs, n == 0, n == len(terms) - 1)
                        scored = pe.mark()
                        s2 = ps[:, 2 * b:2 * b + 2, :]
                        phi = p16[:, b, :].rearrange("p (a b) -> p a b", a=2)
                        plo = p16[:, 2 + b, :].rearrange("p (a b) -> p a b", a=2)
                        act.wait(scored)
                        if p_free[b]:
                            act.wait(p_free[b])
                        exp(phi, s2)
                        exp(s2, s2)
                        exped = act.mark()
                        dve.wait(exped)
                        if p_free[b]:
                            dve.wait(p_free[b])
                        tt(dve, plo, s2, phi, ALU.subtract)
                        low = dve.mark()
                        sc_free[b] = low
                    if pending is not None:
                        tb, tslot, tready, tlow, tt_ = pending
                        pe.wait(tready, tlow)
                        if tt_ == 0:
                            pe.wait(*att_ready)
                        for h in range(8):
                            o = ps[:, 4 + h // 2, (h % 2) * 256:(h % 2) * 256 + C + 2]
                            first = tt_ == 0 and h % 2 == 0
                            c16t = ctx16[:, tslot, tt_ % CH, :]
                            kw = dict(skip_group_check=True)
                            hh = slice(h * P, (h + 1) * P)
                            mm(o, p16[:, tb, hh], c16t[:, 0:LO], first, False, **kw)
                            mm(o[:, 0:C], p16[:, tb, hh], c16t[:, LO:NW], False, False, **kw)
                            mm(o, p16[:, 2 + tb, hh], c16t[:, 0:LO], False, tt_ == NT - 1, **kw)
                        p_free[tb] = pe.mark()
                        if tt_ % CH == CH - 1:
                            read_done[tslot] = (p_free[tb],)
                    pending = (b, slot, chunk_ready, low, t) if t < NT else None
                summed = p_free[(NT - 1) % 2]
                inv = small[:, 224:232]
                o4 = ps[:, 4:8, :].rearrange("p a (b c) -> p a b c", b=2)
                dve.wait(summed)
                reciprocal(inv.rearrange("p (a b) -> p a b", b=2), o4[:, :, :, ONE])
                dve.settle()
                for k in range(2):
                    if att_ready:
                        dve.wait(*att_ready)
                    tt(dve, U[:, :, :].rearrange("p (a b) c -> p a b c", a=2), o4[:, 2 * k:2 * k + 2, :, 0:C],
                       bc(inv[:, 4 * k:4 * k + 4].rearrange("p (a b) -> p a b", b=2), 3, [P, 2, 2, C]), ALU.mult)
                    u_ready = dve.mark()
                    pe.wait(u_ready)
                    for j in range(4):
                        tp(ps[:, 0, j * P:(j + 1) * P], U[:, j, 0:P], ident[:, :])
                        tp(ps[0:CB_ROW, 1, j * P:(j + 1) * P], U[:, j, P:C], ident[:, :])
                    turned = pe.mark()
                    act.wait(turned)
                    copy(act, uT_a[:, :], ps[:, 0, :])
                    a_ready = act.mark()
                    dve.wait(turned)
                    copy(dve, uT_b[:, :], ps[0:CB_ROW, 1, :])
                    b_ready = dve.mark()
                    pe.wait(a_ready, b_ready, L.wv_ready)
                    for j in range(4):
                        h = g * 8 + k * 4 + j
                        hs = slice(h * L.dh, (h + 1) * L.dh)
                        o = ps[:, 2, j * L.dh:(j + 1) * L.dh]
                        mm(o, uT_a[:, j * P:(j + 1) * P], wvA[:, hs], True, False)
                        mm(o, uT_b[:, j * P:(j + 1) * P], wvB[:, hs], False, True)
                    projected = pe.mark()
                    act.wait(projected)
                    h0 = (g * 8 + k * 4) * L.dh
                    copy(act, att[:, h0:h0 + 4 * L.dh], ps[:, 2, 0:4 * L.dh])
                    att_ready = (act.mark(),)
            return att_ready

        xnT_ready = layernorm((x_in,))
        evacuated = [(), ()]
        act.wait(cols_ready)
        evacuated[0] = evacuated[1] = (xnT_ready,)
        ctxT_ready = [build_ctxT(c) for c in range(NCH)]
        load_split(ld_w2, L0.wv, d["L0_xattn_Wv"], L0.inner)
        ld_w2.load(sp, wview(W1_OFF, 2, 512), d["L0_xattn_W1"].rearrange("(a p) n -> p a n", p=P))
        ld_w2.load(sp, wview(W2_OFF, 4, D), d["L0_xattn_W2"].rearrange("(a p) n -> p a n", p=P))
        ld_w2.load(sp, wview(CA_OFF, 2, 3 * D), d["L0_attn_c_attn_w"].rearrange("(a p) n -> p a n", p=P))
        L0.wv_ready = ld_w2.load(sp, wview(CP_OFF, 2, D), d["L0_attn_c_proj_w"].rearrange("(a p) n -> p a n", p=P))
        pe.wait(*(evacuated[0] + evacuated[1]), xnT_ready, cols_ready)
        dve.wait(cols_ready)
        att_ready = xattn(L0, l0_proj_in, "L0_xattn_bq", "L0_xattn_bk", xnT_ready)

        attT = scratch[:, 0:2 * P].rearrange("p (a q) -> p a q", a=2)
        hT = scratch[:, 256:256 + 4 * P].rearrange("p (a q) -> p a q", a=4)
        pe.wait(*att_ready)
        for i in range(2):
            tp(ps[:, 0, i * P:(i + 1) * P], att[:, i * P:(i + 1) * P], ident[:, :])
        turned = pe.mark()
        dve.wait(turned)
        for i in range(2):
            ts(dve, attT[:, i, :], ps[:, 0, i * P:(i + 1) * P], col("L0_xattn_bv", i), None, ALU.add)
        ready = dve.mark()
        pe.wait(ready)
        w1, w2 = wview(W1_OFF, 2, 512), wview(W2_OFF, 4, D)
        for f in range(4):
            for a in range(2):
                mm(ps[:, 1, f * P:(f + 1) * P], w1[:, a, f * P:(f + 1) * P], attT[:, a, :], a == 0, a == 1)
        ready = pe.mark()
        dve.wait(ready)
        for f in range(4):
            ts(dve, hT[:, f, :], ps[:, 1, f * P:(f + 1) * P], col("L0_xattn_b1", f), 0.0, ALU.add, ALU.max)
        ready = dve.mark()
        pe.wait(ready)
        for f in range(4):
            mm(ps[:, 2, 0:D], hT[:, f, :], w2[:, f, :], f == 0, False)
        mm(ps[:, 2, 0:D], row_select(BR["L0_xattn_b2"]), bias_rows[:, :], False, True)
        x_ready = residual(ps[:, 2, 0:D], pe.mark())

        xnT_ready = layernorm(())
        ca, cp = wview(CA_OFF, 2, 3 * D), wview(CP_OFF, 2, D)
        qkT = scratch[:, 0:512].rearrange("p (a q) -> p a q", a=4)
        v_tok = scratch[:, 512:768]
        spread = scratch[:, 768:768 + 2048].rearrange("p (h q) -> p h q", h=H)
        probT = scratch[:, 768:768 + 2048].rearrange("p (h q) -> p h q", h=H)
        prob = scratch[:, 2816:2816 + 2048].rearrange("p (h q) -> p h q", h=H)
        pe.wait(xnT_ready)
        for n in range(4):
            for a in range(2):
                mm(ps[:, 1, n * P:(n + 1) * P], ca[:, a, n * P:(n + 1) * P], xnT[:, a, :], a == 0, a == 1)
        qk_in = pe.mark()
        for a in range(2):
            mm(ps[:, 2, 0:D], xnT[:, a, :], ca[:, a, 2 * D:3 * D], a == 0, False)
        mm(ps[:, 2, 0:D], row_select(BR["L0_attn_c_attn_b"]), bias_rows[:, :], False, True)
        v_in = pe.mark()
        dve.wait(qk_in)
        for n in range(4):
            ts(dve, qkT[:, n, :], ps[:, 1, n * P:(n + 1) * P], col("L0_attn_c_attn_b", n),
               0.25 if n < 2 else 1.0, ALU.add, ALU.mult)
        dve.settle()
        for i in range(2):
            tt(dve, spread[:, 8 * i:8 * i + 8, :], bc(qkT[:, i, :], 1, [P, 8, P]),
               bc(head16[:, :], 2, [P, 8, P]), ALU.mult)
        spread_ready = dve.mark()
        act.wait(v_in)
        copy(act, v_tok, ps[:, 2, 0:D])
        v_ready = act.mark()
        pe.wait(spread_ready)
        sc = ps[:, 4:8, :]
        for b in range(4):
            mm(ps[:, 4 + b, :], ident[:, :], bc(causal[:, :], 1, [P, 4, P]), True, False, skip_group_check=True)
            for j in range(4):
                h = 4 * b + j
                mm(ps[:, 4 + b, j * P:(j + 1) * P], spread[:, h, :], qkT[:, 2 + h // 8, :], False, True,
                   skip_group_check=True)
        scored = pe.mark()
        mx, tot = small[:, 16:32], small[:, 32:48]
        sch = sc.rearrange("p b (j q) -> p b j q", j=4)

        def by4(t):
            return t.rearrange("p (b j) -> p b j", b=4)

        dve.wait(scored)
        reduce(by4(mx), sch, AX.X, ALU.max).settle()
        tt(dve, prob.rearrange("p (b j) q -> p b j q", b=4), sch, bc(by4(mx), 3, [P, 4, 4, P]), ALU.subtract)
        centred = dve.mark()
        act.wait(centred)
        exp(prob, prob)
        exped = act.mark()
        dve.wait(exped)
        reduce(tot, prob, AX.X, ALU.add).settle()
        reciprocal(tot, tot).settle()
        pe.wait(exped)
        for h in range(H):
            tp(ps[:, h // 4, (h % 4) * P:(h % 4 + 1) * P], prob[:, h, :], ident[:, :])
        turned = pe.mark()
        act.wait(turned)
        copy(act, probT[:, 0:8, :].rearrange("p (b j) q -> p b (j q)", b=2), ps[:, 0:2, :])
        t1 = act.mark()
        dve.wait(turned)
        copy(dve, probT[:, 8:16, :].rearrange("p (b j) q -> p b (j q)", b=2), ps[:, 2:4, :])
        t2 = dve.mark()
        pe.wait(t1, t2, v_ready)
        for h in range(H):
            mm(ps[:, 4, h * 16:(h + 1) * 16], probT[:, h, :], v_tok[:, h * 16:(h + 1) * 16], True, True)
        ready = pe.mark()
        dve.wait(ready)
        tt(dve, att[:, 0:D].rearrange("p (h d) -> p h d", h=H), ps[:, 4, 0:D].rearrange("p (h d) -> p h d", h=H),
           bc(tot, 2, [P, H, 16]), ALU.mult)
        ready = dve.mark()
        attT_ready = transpose_act(att, 2, attT, (ready,), 5)
        pe.wait(attT_ready)
        for a in range(2):
            mm(ps[:, 6, 0:D], attT[:, a, :], cp[:, a, :], a == 0, False)
        mm(ps[:, 6, 0:D], row_select(BR["L0_attn_c_proj_b"]), bias_rows[:, :], False, True)
        x_ready = residual(ps[:, 6, 0:D], pe.mark())

        def gate(logits, ready, second_softmax):
            pr, w, mxe, tot = small[:, 240:248], small[:, 248:256], small[:, 256:257], small[:, 257:258]
            rank = small[:, 264:272]
            grid, eq = small[:, 320:384], small[:, 384:448]
            g3, q3 = (t.rearrange("p (e j) -> p e j", e=NE) for t in (grid, eq))
            dve.wait(ready)
            reduce(mxe, logits, AX.X, ALU.max).settle()
            ts(dve, pr, logits, mxe, None, ALU.subtract)
            t = dve.mark()
            act.wait(t)
            exp(pr, pr)
            t = act.mark()
            dve.wait(t)
            reduce(tot, pr, AX.X, ALU.add).settle()
            reciprocal(tot, tot).settle()
            ts(dve, pr, pr, tot, None, ALU.mult)
            dve.settle()
            pj, pe_ = bc(pr, 1, [P, NE, NE]), bc(pr, 2, [P, NE, NE])
            tt(dve, g3, pj, pe_, ALU.is_gt)
            tt(dve, q3, pj, pe_, ALU.is_equal)
            dve.settle()
            tt(dve, q3, q3, lower[:, :, :], ALU.mult)
            dve.settle()
            tt(dve, g3, g3, q3, ALU.add)
            dve.settle()
            reduce(rank, g3, AX.X, ALU.add).settle()
            ts(dve, rank, rank, 1.5, None, ALU.is_lt)
            if second_softmax:
                reduce(mxe, pr, AX.X, ALU.max).settle()
                ts(dve, pr, pr, mxe, None, ALU.subtract)
                t = dve.mark()
                act.wait(t)
                exp(pr, pr)
                t = act.mark()
                dve.wait(t)
            else:
                dve.settle()
            tt(dve, w, pr, rank, ALU.mult)
            dve.settle()
            reduce(tot, w, AX.X, ALU.add).settle()
            if not second_softmax:
                ts(dve, tot, tot, 1e-6, None, ALU.add)
                dve.settle()
            reciprocal(tot, tot).settle()
            ts(dve, w, w, tot, None, ALU.mult)
            dve.settle()
            return w

        xnT_ready = layernorm(())
        bias2 = scratch[0:8, 4608:4608 + D]
        wg = scratch[:, 4864:4864 + 2 * NE].rearrange("p (a n) -> p a n", a=2)
        sp.wait(x_ready)
        ld_bias.load(sp, wg, d["L0_ffn_Wg"].rearrange("(a p) n -> p a n", p=P))
        gate_in = ld_bias.load(sp, bias2, d["L0_ffn_b2"])
        slot_free = [(x_ready,), (x_ready,)]

        def load_expert0(e):
            off = 4096 * (e % 2)
            sp.wait(*slot_free[e % 2])
            ld_exp[e % 2].load(sp, wview(off, 2, F0), d["L0_ffn_W1"][e].rearrange("(a p) n -> p a n", p=P))
            return ld_exp[e % 2].load(sp, wview(off + 2048, F0 // P, D),
                                      d["L0_ffn_W2"][e].rearrange("(a p) n -> p a n", p=P))

        loaded = [load_expert0(0), load_expert0(1)]
        pe.wait(xnT_ready, gate_in)
        for a in range(2):
            mm(ps[:, 1, 0:NE], xnT[:, a, :], wg[:, a, :], a == 0, False)
        mm(ps[:, 1, 0:NE], row_select(BR["L0_ffn_bg"]), bias_rows[:, 0:NE], False, True)
        w_e = gate(ps[:, 1, 0:NE], pe.mark(), False)
        w_ready = dve.mark() if dve.steps[-1][1] is None else (dve.sem, dve.count)
        wT = scratch[0:8, 4480:4480 + P]
        pe.wait(w_ready)
        tp(ps[0:8, 2, 0:P], w_e, ident[:, :])
        t = pe.mark()
        act.wait(t)
        copy(act, wT, ps[0:8, 2, 0:P])
        t = act.mark()
        pe.wait(t)
        mm(ps[:, 1, 0:D], wT, bias2, True, True)
        residual(ps[:, 1, 0:D], pe.mark())
        NF = F0 // P
        hT2 = [scratch[:, 2048 * 0 + 1024 * n:1024 * (n + 1)].rearrange("p (f q) -> p f q", f=NF) for n in range(2)]
        h_free, y_free, hidden = [None, None], [None, None], [None, None]

        def hidden0(e_):
            b = e_ % 2
            w1 = wview(4096 * b, 2, F0)
            pe.wait(loaded[e_])
            if hidden[b]:
                pe.wait(hidden[b])
            for k in range(NF // 4):
                bank = 2 + 2 * b + k
                for j in range(4):
                    f = 4 * k + j
                    for a in range(2):
                        mm(ps[:, bank, j * P:(j + 1) * P], w1[:, a, f * P:(f + 1) * P], xnT[:, a, :], a == 0, a == 1)
                summed = pe.mark()
                act.wait(summed)
                if h_free[b]:
                    act.wait(h_free[b])
                for j in range(4):
                    gelu(hT2[b][:, 4 * k + j, :], ps[:, bank, j * P:(j + 1) * P], col("L0_ffn_b1", e_ * NF + 4 * k + j))
            hidden[b] = act.mark()

        def down0(e_):
            b = e_ % 2
            w2 = wview(4096 * b + 2048, NF, D)
            pe.wait(hidden[b])
            if y_free[b]:
                pe.wait(y_free[b])
            for f in range(NF):
                mm(ps[:, 6 + b, 0:D], hT2[b][:, f, :], w2[:, f, :], f == 0, f == NF - 1)
            y = pe.mark()
            h_free[b] = y
            slot_free[b] = (y,)
            dve.wait(y)
            weigh(ps[:, 6 + b, 0:D], w_e[:, e_:e_ + 1])
            y_free[b] = dve.settle()

        for e_ in range(NE + 1):
            if e_ < NE:
                hidden0(e_)
            if e_:
                down0(e_ - 1)
                if e_ + 1 < NE:
                    loaded.append(load_expert0(e_ + 1))
        x_ready = y_free[(NE - 1) % 2]

        sp.wait(x_ready)
        ld_w.load(sp, wview(L1.wq, 2, L1.inner), d["L1_xattn_Wq"].rearrange("(a p) n -> p a n", p=P))
        l1_proj_in = load_split(ld_w, L1.wk, d["L1_xattn_Wk"], L1.inner)
        load_split(ld_w2, L1.wv, d["L1_xattn_Wv"], L1.inner)
        L1.wv_ready = ld_w2.load(sp, wview(L1.wo, 8, D), d["L1_xattn_Wo"].rearrange("(a p) n -> p a n", p=P))
        xnT_ready = layernorm(())
        dve.do(lambda e: e.memset(q_c[CB_ROW:P, :], 0.0))
        dve.do(lambda e: e.memset(q_m[CB_ROW:P, :], 0.0)).settle()
        act.wait((dve.sem, dve.count))
        att_ready = xattn(L1, l1_proj_in, None, None, xnT_ready)
        attT = scratch[:, 0:1024].rearrange("p (a q) -> p a q", a=8)
        attT_ready = transpose_act(att, 8, attT, att_ready, 4)
        wo = wview(L1.wo, 8, D)
        pe.wait(attT_ready)
        for a in range(8):
            mm(ps[:, 3, 0:D], attT[:, a, :], wo[:, a, :], a == 0, False)
        mm(ps[:, 3, 0:D], row_select(BR["L1_xattn_bo"]), bias_rows[:, :], False, True)
        x_ready = residual(ps[:, 3, 0:D], pe.mark())

        sp.wait(x_ready)
        wa = scratch[:, 4096:4608].rearrange("p (a n) -> p a n", a=2)
        wr = scratch[:, 4608:4608 + 2 * NE].rearrange("p (a n) -> p a n", a=2)
        ld_bias.load(sp, wa, d["L1_attn_W"].rearrange("(a p) n -> p a n", p=P))
        gate_in = ld_bias.load(sp, wr, d["L1_ffn_router_kernel_DE"].rearrange("(a p) n -> p a n", p=P))
        slot_free = [(x_ready,), (x_ready,)]
        NF1 = F1 // P

        def load_expert1(e):
            off = 3072 * (e % 2)
            sp.wait(*slot_free[e % 2])
            ld_exp[e % 2].load(sp, wview(off, 2, F1), d["L1_ffn_kernel_gating_EDF"][e].rearrange("(a p) n -> p a n", p=P))
            ld_exp[e % 2].load(sp, wview(off + 1024, 2, F1), d["L1_ffn_kernel_up_EDF"][e].rearrange("(a p) n -> p a n", p=P))
            return ld_exp[e % 2].load(sp, wview(off + 2048, NF1, D),
                                      d["L1_ffn_kernel_down_EFD"][e].rearrange("(a p) n -> p a n", p=P))

        loaded = [load_expert1(0), load_expert1(1)]

        xnT_ready = layernorm(())
        prob, mask = scratch[:, 0:128], scratch[:, 128:256]
        mx, tot, vac, spr = small[:, 16:17], small[:, 17:18], small[:, 18:19], small[:, 19:20]
        wsum = small[:, 20:22]
        pe.wait(xnT_ready)
        for a in range(2):
            mm(ps[:, 1, 0:P], xnT[:, a, :], xnT[:, a, :], a == 0, a == 1)
        scored = pe.mark()
        dve.wait(scored, x_ready)
        reduce(mx, ps[:, 1, 0:P], AX.X, ALU.max).settle()
        ts(dve, prob, ps[:, 1, 0:P], mx, 1.0 / 16, ALU.subtract, ALU.mult)
        t = dve.mark()
        act.wait(t)
        exp(prob, prob)
        t = act.mark()
        dve.wait(t)
        reduce(tot, prob, AX.X, ALU.add).settle()
        reciprocal(tot, tot).settle()
        ts(dve, prob, prob, tot, None, ALU.mult)
        dve.settle()
        ts(dve, mask, prob, 0.01, None, ALU.is_lt)
        dve.settle()
        tt(dve, mask, mask, prob, ALU.mult)
        dve.settle()
        reduce(vac, mask, AX.X, ALU.add)
        tt(dve, prob, prob, mask, ALU.subtract)
        dve.settle()
        reduce(spr, prob, AX.X, ALU.add).settle()
        ts(dve, spr, spr, 1e-9, None, ALU.add)
        dve.settle()
        reciprocal(spr, spr).settle()
        ts(dve, prob, prob, spr, None, ALU.mult)
        dve.wait(gate_in)
        reduce(wsum, wa, AX.X, ALU.add).settle()
        ts(dve, wsum, wsum, 0.01, None, ALU.mult)
        t = dve.mark()
        pe.wait(t)
        tp(ps[:, 2, 0:P], prob, ident[:, :])
        tp(ps[0:1, 2, P:2 * P], vac, ident[:, :])
        for a in range(2):
            tp(ps[0:1, 2, (2 + a) * P:(3 + a) * P], wsum[:, a:a + 1], ident[:, :])
        t = pe.mark()
        act.wait(t)
        probT = scratch[:, 256:384]
        rows = scratch[0:1, 384:384 + 384]
        copy(act, probT, ps[:, 2, 0:P])
        copy(act, rows, ps[0:1, 2, P:4 * P])
        t = act.mark()
        pe.wait(t)
        mm(ps[:, 3, 0:D], probT, xn[:, :], True, False)
        mm(ps[:, 3, 0:D], rows[:, 0:P], rows[:, P:3 * P], False, True)
        x_ready = residual(ps[:, 3, 0:D], pe.mark())

        xnT_ready = layernorm(())
        pe.wait(xnT_ready, gate_in)
        for a in range(2):
            mm(ps[:, 1, 0:NE], xnT[:, a, :], wr[:, a, :], a == 0, a == 1)
        w_e = gate(ps[:, 1, 0:NE], pe.mark(), True)
        fuse = [scratch[:, 1024 * n:1024 * n + NF1 * P].rearrange("p (f q) -> p f q", f=NF1) for n in range(2)]
        sig = [scratch[:, 1024 * n + 512:1024 * n + 512 + NF1 * P] for n in range(2)]
        h_free, y_free, fused = [None, None], [None, None], [None, None]

        def hidden1(e_):
            b = e_ % 2
            wgt, wup = wview(3072 * b, 2, F1), wview(3072 * b + 1024, 2, F1)
            gp, up = ps[:, 2 + 2 * b, :], ps[:, 3 + 2 * b, :]
            pe.wait(loaded[e_])
            if fused[b]:
                pe.wait(fused[b])
            made = []
            for o, w in ((gp, wgt), (up, wup)):
                for f in range(NF1):
                    for a in range(2):
                        mm(o[:, f * P:(f + 1) * P], w[:, a, f * P:(f + 1) * P], xnT[:, a, :], a == 0, a == 1)
                made.append(pe.mark())
            act.wait(made[0])
            if fused[b]:
                act.wait(fused[b])
            exp(sig[b], gp, scale=-1.0)
            exped = act.mark()
            dve.wait(exped)
            ts(dve, sig[b], sig[b], 1.0, None, ALU.add)
            dve.settle()
            reciprocal(sig[b], sig[b]).settle()
            tt(dve, sig[b], gp, sig[b], ALU.mult)
            dve.settle()
            dve.wait(made[1])
            if h_free[b]:
                dve.wait(h_free[b])
            tt(dve, fuse[b].rearrange("p f q -> p (f q)"), up, sig[b], ALU.mult)
            fused[b] = dve.mark()

        def down1(e_):
            b = e_ % 2
            wdn = wview(3072 * b + 2048, NF1, D)
            pe.wait(fused[b])
            if y_free[b]:
                pe.wait(y_free[b])
            for f in range(NF1):
                mm(ps[:, 6 + b, 0:D], fuse[b][:, f, :], wdn[:, f, :], f == 0, f == NF1 - 1)
            y = pe.mark()
            h_free[b] = y
            slot_free[b] = (y,)
            dve.wait(y)
            weigh(ps[:, 6 + b, 0:D], w_e[:, e_:e_ + 1])
            y_free[b] = dve.settle()

        for e_ in range(NE + 1):
            if e_ < NE:
                hidden1(e_)
            if e_:
                down1(e_ - 1)
                if e_ + 1 < NE:
                    loaded.append(load_expert1(e_ + 1))
        sp.wait(y_free[(NE - 1) % 2])
        sp.wait(st_out.load(sp, out[0], x[:, :]))

        block = ctx.enter_context(nc.Block())
        block.tensor(pe.run)
        block.scalar(act.run)
        block.vector(dve.run)
        block.gpsimd(pool.run)
        block.sync(sp.run)


_OUTS = [((1, 128, 256), "float32")]


def kernel(**inputs):
    import numpy as _np
    import concourse.bacc as _bacc
    from concourse import mybir as _mybir
    from concourse.bass_utils import run_bass_kernel_spmd as _run

    nc = _bacc.Bacc("TRN2", target_bir_lowering=False, num_devices=1)
    arrays, args = {}, {}
    for name in inputs:
        a = _np.ascontiguousarray(inputs[name])
        arrays[f"in_{name}_dram"] = a
        args[name] = nc.dram_tensor(f"in_{name}_dram", a.shape, _mybir.dt.from_np(a.dtype), kind="ExternalInput").ap()
    shape, dtype = _OUTS[0]
    out = nc.dram_tensor("out_0_dram", shape, _mybir.dt.from_np(_np.dtype(dtype)), kind="ExternalOutput").ap()
    perceiver_kernel(nc, args, out)
    r = _run(nc, [arrays], core_ids=[0])
    return r.results[0]["out_0_dram"]
```

```python
from contextlib import ExitStack

import concourse.bass as bass
from concourse import mybir

F32 = mybir.dt.float32
F16 = mybir.dt.float16
ALU = mybir.AluOpType
ACT = mybir.ActivationFunctionType
AX = mybir.AxisListType

P = 128
EPS = 1e-5
EXP_SHIFT = 8 * 0.6931471805599453


class Queue:

    def __init__(self, sem):
        self.sem, self.count, self.steps, self.known = sem, 0, [], {}

    def do(self, build):
        self.steps.append([build, None])
        return self

    def mark(self):
        assert self.steps[-1][1] is None
        self.count += 1
        self.steps[-1][1] = self.sem
        return (self.sem, self.count)

    def wait(self, *tokens):
        for sem, value in tokens:
            if self.known.get(sem.name, 0) < value:
                self.known[sem.name] = value
                self.steps.append([lambda e, s=sem, v=value: e.wait_ge(s, v), "wait"])
        return self

    def settle(self):
        token = self.mark()
        self.wait(token)
        return token

    def run(self, engine):
        for build, sem in self.steps:
            ins = build(engine)
            if sem is not None and sem != "wait":
                ins.then_inc(sem, 1)


class Landing:

    def __init__(self, sem):
        self.sem, self.total = sem, 0

    def load(self, queue, out, in_):
        self.total += 16
        queue.steps.append([lambda e, o=out, i=in_, s=self.sem: e.dma_start(o, i).then_inc(s, 16), "wait"])
        return (self.sem, self.total)


def perceiver_kernel(nc, d, out):
    _, N_TOK, D = d["x"].shape
    _, M, C = d["ctx_768"].shape
    H = 16
    NE = d["L0_ffn_Wg"].shape[1]
    F0 = d["L0_ffn_W1"].shape[2]
    F1 = d["L1_ffn_kernel_gating_EDF"].shape[2]
    assert N_TOK == P and D == 2 * P and C == 192 and M % P == 0
    NT = M // P
    CH = 7
    NCH = NT // CH
    assert NT % CH == 0
    CW = CH * C
    VS = 32.0
    MAXC = 448
    MAXB = 2
    NMAX = M // (MAXC * MAXB)
    assert NMAX * MAXC * MAXB == M
    DIRECT = (2, 5, 8, 11)
    CB_ROW = C - P
    R_ROW, C_ROW, K_C = 64, 66, 68

    ctx = ExitStack()
    with ctx:
        def sb(name, shape, dt):
            return ctx.enter_context(nc.sbuf_tensor(name, shape, dt))

        def sem(name):
            return ctx.enter_context(nc.semaphore(name))

        ctxT_a_hi = sb("ctxT_a_hi", [P, M], F16)
        ctxT_a_lo = sb("ctxT_a_lo", [P, M], F16)
        ctxT_b = sb("ctxT_b", [P, M], F16)
        ctxT_c = sb("ctxT_c", [P, M], F16)
        q_all = sb("q_all", [P, 5, H * P], F16)
        q_a_hi, q_a_lo, q_b, q_c, q_m = (q_all[:, n, :] for n in range(5))
        scratch = q_all[:, :, :].rearrange("p a b -> p (a b)").bitcast(F32)
        p16 = sb("p16", [P, 4, 8 * P], F16)
        stage = sb("stage", [P, 2 * CW + 2 * CW], F32)
        ctx32 = stage[:, 0:2 * CW].rearrange("p (s n) -> p s n", s=2)
        ctx16 = stage[:, 2 * CW:4 * CW].bitcast(F16).rearrange("p (s t c) -> p s t c", s=2, t=CH)
        tail = stage[:, 4096:4 * CW]
        bias2 = tail[0:8, 0:D]
        wg = tail[:, 256:272].rearrange("p (a n) -> p a n", a=2)
        bias_rows = tail[0:8, 784:784 + D]
        wv16 = sb("wv16", [P, 4, 1024], F16)
        v16 = sb("v16", [P, 2, 8 * 130], F16)
        W = sb("W", [P, 9744], F32)
        x = sb("x_tok", [P, D], F32)
        xn = sb("xn", [P, D], F32)
        xnT = sb("xnT", [P, 2, P], F32)
        att = sb("att", [P, 1024], F32)
        ident = sb("ident", [P, P], F32)
        ident16 = sb("ident16", [P, P], F16)
        causal = sb("causal", [P, P], F32)
        head16 = sb("head16", [P, 8], F32)
        head64 = sb("head64", [P, 2], F32)
        lower = sb("lower", [P, NE, NE], F32)
        cols = sb("cols", [P, P], F32)
        small = sb("small", [P, 400], F32)
        minus_half = sb("minus_half", [P, 1], F32)
        ps = ctx.enter_context(nc.psum_tensor("ps", [P, 8, 512], F32))

        def row_select(n):
            return ident[0:8, n:n + 1].to_broadcast([8, P])

        pe, act, dve, pool, sp = (Queue(sem(f"{n}_done")) for n in ("pe", "act", "dve", "pool", "sp"))
        ld_x = Landing(sem("ld_x"))
        ld_bias = Landing(sem("ld_bias"))
        ld_w = Landing(sem("ld_w"))
        ld_w2 = Landing(sem("ld_w2"))
        ld_exp = [Landing(sem(f"ld_exp{n}")) for n in range(3)]
        ld_ctx = [Landing(sem(f"ld_ctx{n}")) for n in range(2)]
        ld_rows = Landing(sem("ld_rows"))
        st_out = Landing(sem("st_out"))

        def mm(out, lhsT, rhs, start, stop, **kw):
            pe.do(lambda e: e.matmul(out, lhsT, rhs, start=start, stop=stop, **kw))

        def tp(out, in_, idt):
            pe.do(lambda e: e.transpose(out, in_, idt))

        def copy(q, out, in_):
            if q is act:
                q.do(lambda e: e.copy(out, in_))
            else:
                q.do(lambda e: e.tensor_copy(out, in_))

        def tt(q, out, a, b, op):
            q.do(lambda e: e.tensor_tensor(out, a, b, op))

        def ts(q, out, a, s1, s2, op0, op1=None):
            if op1 is None:
                q.do(lambda e: e.tensor_scalar(out, a, s1, None, op0))
            else:
                q.do(lambda e: e.tensor_scalar(out, a, s1, s2, op0, op1))

        def reduce(out, in_, axis, op):
            return dve.do(lambda e: e.tensor_reduce(out, in_, axis, op))

        def reciprocal(out, in_):
            return dve.do(lambda e: e.reciprocal(out, in_))

        def exp(out, in_, scale=1.0):
            act.do(lambda e: e.activation(out, in_, ACT.Exp, scale=scale))

        def scaled(out, in_):
            act.do(lambda e: e.mul(out, in_, VS))

        def clear(out, value):
            dve.do(lambda e: e.memset(out, value))

        def gelu(out, in_, bias):
            act.do(lambda e: e.activation(out, in_, ACT.Gelu_apprx_tanh, bias=bias))

        def weigh(y, w):
            dve.do(lambda e: e.scalar_tensor_tensor(out=x[:, :], in0=y, scalar=w, in1=x[:, :],
                                                    op0=ALU.mult, op1=ALU.add))

        def bc(ap, axis, shape):
            return ap.unsqueeze(axis).to_broadcast(shape)

        def layernorm(ready, bank=0):
            stats, mv, rstd = small[:, 0:6], small[:, 6:8], small[:, 8:9]
            dve.wait(*ready)
            dve.do(lambda e: e.bn_stats(stats, x[:, :])).settle()
            dve.do(lambda e: e.bn_aggr(mv, stats)).settle()
            ts(dve, rstd, mv[:, 1:2], EPS, None, ALU.add)
            var_ready = dve.mark()
            pool.wait(var_ready)
            tt(pool, rstd, rstd, minus_half[:, :], ALU.pow)
            rstd_ready = pool.mark()
            dve.wait(rstd_ready)
            ts(dve, xn[:, :], x[:, :], mv[:, 0:1], rstd, ALU.subtract, ALU.mult)
            normed = dve.mark()
            pe.wait(normed)
            for i in range(2):
                tp(ps[:, bank, i * P:(i + 1) * P], xn[:, i * P:(i + 1) * P], ident[:, :])
            turned = pe.mark()
            act.wait(turned)
            copy(act, xnT[:, :, :], ps[:, bank, 0:2 * P].rearrange("p (a b) -> p a b", a=2))
            return act.mark()

        def residual(y, ready):
            dve.wait(ready)
            tt(dve, x[:, :], y, x[:, :], ALU.add)
            return dve.settle()

        def transpose_act(src, n, dst, ready, bank, idt=None):
            pe.wait(*ready)
            for i in range(n):
                tp(ps[:, bank + i // 4, (i % 4) * P:(i % 4 + 1) * P], src[:, i * P:(i + 1) * P], ident[:, :])
            turned = pe.mark()
            act.wait(turned)
            nb = -(-n // 4)
            w = min(n, 4) * P
            copy(act, dst.rearrange("p (b i) q -> p b (i q)", b=nb), ps[:, bank:bank + nb, 0:w])
            return act.mark()

        pool.do(lambda e: e.memset(ident[:, :], 0.0))
        pool.do(lambda e: e.memset(causal[:, :], 0.0))
        pool.do(lambda e: e.memset(minus_half[:, :], -0.5))
        pool.do(lambda e: e.memset(head16[:, :], 1.0))
        pool.do(lambda e: e.memset(head64[:, :], 1.0))
        pool.do(lambda e: e.memset(lower[:, :, :], 1.0)).settle()
        pool.do(lambda e: e.affine_select(out=ident[:, :], in_=ident[:, :], compare_op=ALU.not_equal,
                                          fill=1.0, base=0, pattern=[[-1, P]], channel_multiplier=1))
        pool.do(lambda e: e.affine_select(out=causal[:, :], in_=causal[:, :], compare_op=ALU.is_ge,
                                          fill=-1e10, base=0, pattern=[[-1, P]], channel_multiplier=1))
        for t, n, w in ((head16, 8, 16), (head64, 2, 64)):
            pool.do(lambda e, t=t, n=n, w=w: e.affine_select(
                out=t[:, :], in_=t[:, :], compare_op=ALU.is_ge, fill=0.0, base=0,
                pattern=[[-w, n]], channel_multiplier=1))
        pool.settle()
        for t, n, w in ((head16, 8, 16), (head64, 2, 64)):
            pool.do(lambda e, t=t, n=n, w=w: e.affine_select(
                out=t[:, :], in_=t[:, :], compare_op=ALU.is_ge, fill=0.0, base=w - 1,
                pattern=[[w, n]], channel_multiplier=-1))
        pool.do(lambda e: e.affine_select(out=lower[:, :, :], in_=lower[:, :, :], compare_op=ALU.is_ge,
                                          fill=0.0, base=-1, pattern=[[1, NE], [-1, NE]],
                                          channel_multiplier=0))
        constants = pool.mark()
        dve.do(lambda e: e.memset(ctxT_c[CB_ROW:P, :], 1.0))
        dve.do(lambda e: e.memset(q_c[CB_ROW:P, :], 0.0))
        dve.do(lambda e: e.memset(q_m[CB_ROW:P, :], 0.0))
        col_in = att[:, 0:P]
        dve.do(lambda e: e.memset(col_in, 0.0))
        blank = dve.mark()
        dve.wait(constants)
        copy(dve, ident16[:, :], ident[:, :])
        ident16_ready = dve.mark()

        x_in = ld_x.load(sp, x[:, :], d["x"][0])
        sp.wait(blank)
        CL, row = {}, 0
        for name, n in (("L0_xattn_bq", 2), ("L0_xattn_bk", 2), ("L0_xattn_bv", 2), ("L0_xattn_b1", 4),
                        ("L0_attn_c_attn_b", 4)):
            CL[name] = row
            biases_in = ld_bias.load(sp, col_in[row:row + n, :],
                                     d[name].rearrange("(r n) -> r n", n=P)[0:n, :])
            row += n
        CL["L0_ffn_b1"] = row
        nb1 = NE * F0 // P
        biases_in = ld_bias.load(sp, col_in[row:row + nb1, :],
                                 d["L0_ffn_b1"].rearrange("e (r n) -> (e r) n", n=P))

        def col(name, i):
            return cols[:, CL[name] + i:CL[name] + i + 1]

        pe.wait(constants, biases_in)
        tp(ps[:, 7, 0:P], col_in, ident[:, :])
        turned = pe.mark()
        act.wait(turned)
        copy(act, cols[:, :], ps[:, 7, 0:P])
        cols_ready = act.mark()
        pe.wait(cols_ready)
        dve.wait(cols_ready)

        def wview(off, a, b):
            return W[:, off:off + a * b].rearrange("p (a b) -> p a b", a=a)

        def by_rows(region, a, n):
            return region[:, 0:a * n].rearrange("p (a n) -> p a n", a=a)

        def load_blocks(landing, region, src):
            a, n = src.shape[0] // P, src.shape[1]
            return landing.load(sp, by_rows(region, a, n), src.rearrange("(a p) n -> p a n", p=P))

        def load_split(landing, region, src):
            n = src.shape[1]
            landing.load(sp, region[:, 0:n], src[0:P, :])
            return landing.load(sp, region[0:CB_ROW, n:2 * n], src[P:C, :])

        class XA:
            pass

        L0 = XA()
        L0.dh, L0.hp, L0.mask, L0.scale = 16, 8, head16, 0.25
        L0.wq, L0.wk, L0.wkT = W[:, 0:512], W[:, 512:1024], W[:, 1024:1536]
        L0.wv = W[:, 1536:2048]
        L0.inner = H * L0.dh
        L0.rows = W[0:1, 0:1024]
        L1 = XA()
        L1.dh, L1.hp, L1.mask, L1.scale = 64, 2, head64, 0.125
        L1.wq, L1.wk, L1.wkT = W[:, 0:2048], W[:, 2048:4096], W[:, 4096:6144]
        L1.wv, L1.wo = stage[:, 0:2048], stage[:, 2048:4096]
        L1.inner = H * L1.dh
        L1.rows = stage[0:1, 0:1024]
        W1_OFF, W2_OFF = 2048, 3072
        CA_OFF = 4096
        cp = tail[:, 272:784].rearrange("p (a n) -> p a n", a=2)

        load_blocks(ld_w, L0.wq, d["L0_xattn_Wq"])
        l0_proj_in = load_split(ld_w, L0.wk, d["L0_xattn_Wk"])

        ctx_dram = d["ctx_768"][0].rearrange("(p t) c -> p (t c)", p=P)
        split_done = [None, None]
        read_done = [None, None]
        halves = {}
        HI_BANK, B_BANK, LO_BANK = (0, 1), (2, 3), 4

        def split_chunk(c):
            slot = c % 2
            if split_done[slot]:
                sp.wait(split_done[slot])
            landed = ld_ctx[slot].load(sp, ctx32[:, slot, :], ctx_dram[:, c * CW:(c + 1) * CW])
            whole = ctx32[:, slot, :].rearrange("p (t c) -> p t c", t=CH)
            hi, lo = ctx16[:, slot, :, 0:C], ctx16[:, slot, :, C:2 * C]
            act.wait(landed)
            if read_done[slot]:
                act.wait(read_done[slot])
            copy(act, hi, whole)
            hi_ready = act.mark()
            low = dve
            low.wait(landed, hi_ready)
            if read_done[slot]:
                low.wait(read_done[slot])
            tt(low, lo, whole, hi, ALU.subtract)
            halves[c] = split_done[slot] = low.mark()

        evac = {}

        def turn_chunk(c):
            slot = c % 2
            banks = (HI_BANK[c % 2], B_BANK[c % 2], LO_BANK)
            hi, b, lo = (ps[:, n, :].bitcast(F16) for n in banks)
            pe.wait(halves[c], ident16_ready)
            if c >= 2:
                pe.wait(*evac[c - 2][0:2])
            for t in range(CH):
                s = slice(t * P, (t + 1) * P)
                tp(hi[:, s], ctx16[:, slot, t, 0:P], ident16[:, :])
            hi_turned = pe.mark()
            for t in range(CH):
                s = slice(t * P, (t + 1) * P)
                tp(b[0:CB_ROW, s], ctx16[:, slot, t, P:C], ident16[:, :])
                tp(b[CB_ROW:P, s], ctx16[:, slot, t, C + P:2 * C], ident16[:, :])
            b_turned = pe.mark()
            if c >= 1:
                pe.wait(evac[c - 1][2])
            for t in range(CH):
                s = slice(t * P, (t + 1) * P)
                tp(lo[:, s], ctx16[:, slot, t, C:C + P], ident16[:, :])
            read_done[slot] = lo_turned = pe.mark()
            s, w = slice(c * CH * P, (c + 1) * CH * P), CH * P
            act.wait(hi_turned)
            copy(act, ctxT_a_hi[:, s], hi[:, 0:w])
            hi_out = act.mark()
            dve.wait(b_turned)
            copy(dve, ctxT_b[:, s], b[:, 0:w])
            b_out = dve.mark()
            dve.wait(lo_turned)
            copy(dve, ctxT_a_lo[:, s], lo[:, 0:w])
            lo_out = dve.mark()
            pool.wait(b_out, blank)
            copy(pool, ctxT_c[0:CB_ROW, s], ctxT_b[0:CB_ROW, s])
            evac[c] = (hi_out, b_out, lo_out, pool.mark())

        def split_wv(L, ready):
            n = L.inner
            wvA, wvB = L.wv[:, 0:n], L.wv[0:CB_ROW, n:2 * n]
            act.wait(ready)
            scaled(wvA, wvA)
            scaled(wvB, wvB)
            got = act.mark()
            dve.wait(got)
            copy(dve, wv16[:, 0, 0:n], wvA)
            copy(dve, wv16[0:CB_ROW, 2, 0:n], wvB)
            copy(dve, wv16[CB_ROW:P, 2, 0:n], wvB)
            dve.settle()
            tt(dve, wv16[:, 1, 0:n], wvA, wv16[:, 0, 0:n], ALU.subtract)
            tt(dve, wv16[0:CB_ROW, 3, 0:n], wvB, wv16[0:CB_ROW, 2, 0:n], ALU.subtract)
            for b in range(2):
                v4 = v_tile(L, b)
                clear(v4[:, :, L.dh:L.dh + 1], 1.0)
                clear(v4[:, :, L.dh + 1:L.dh + 2], 0.0)
            return dve.mark()

        def v_tile(L, b):
            w = 2 * L.dh + 2
            return v16[:, b, 0:8 * w].rearrange("p (h c) -> p h c", h=8)

        def fold_queries(L, wq_ready, bq, bk, xnT_ready, banks):
            nI = L.inner // P
            hp = L.hp
            wq, wkT = by_rows(L.wq, 2, L.inner), by_rows(L.wkT, nI, 256)
            wkA, wkB = L.wk[:, 0:L.inner], L.wk[0:CB_ROW, L.inner:2 * L.inner]
            qT = p16[:, 0, 0:2 * P].bitcast(F32)
            spread = p16[:, 1:3, :].rearrange("p a b -> p (a b)").bitcast(F32)[:, 0:hp * P].rearrange(
                "p (h q) -> p h q", h=hp)
            qbank = banks[0][2]
            pe.wait(wq_ready, constants, xnT_ready)
            wkT_out = []
            for i in range(0, nI, 2):
                bank = banks[(i // 2) % len(banks)][0]
                if i // 2 >= len(banks):
                    pe.wait(wkT_out[-len(banks)])
                for j in range(2):
                    tp(ps[:, bank, j * C:j * C + P], wkA[:, (i + j) * P:(i + j + 1) * P], ident[:, :])
                    tp(ps[:, bank, j * C + P:(j + 1) * C], wkB[:, (i + j) * P:(i + j + 1) * P],
                       ident[0:CB_ROW, 0:CB_ROW])
                turned = pe.mark()
                act.wait(turned)
                src = ps[:, bank, 0:2 * C].rearrange("p (j c) -> p j c", j=2)
                copy(act, wkT[:, i:i + 2, 0:C], src)
                copy(act, wkT[:, i:i + 2, C:256], src[:, :, P:C])
                wkT_out.append(act.mark())
                yield
            pe.wait(wkT_out[-1], xnT_ready)
            folded, q_free, spread_free, rows_in = [], None, None, None
            for i in range(nI):
                if q_free:
                    pe.wait(q_free)
                if bk and folded:
                    pe.wait(folded[-1])
                for a in range(2):
                    mm(ps[:, qbank, 0:P], wq[:, a, i * P:(i + 1) * P], xnT[:, a, :], a == 0, a == 1)
                q_ready = pe.mark()
                dve.wait(q_ready)
                if bq:
                    ts(dve, qT, ps[:, qbank, 0:P], col(bq, i), L.scale, ALU.add, ALU.mult)
                else:
                    ts(dve, qT, ps[:, qbank, 0:P], L.scale, None, ALU.mult)
                q_free = dve.settle()
                if spread_free:
                    dve.wait(spread_free)
                tt(dve, spread, bc(qT, 1, [P, hp, P]), bc(L.mask[:, :], 2, [P, hp, P]), ALU.mult)
                spread_ready = dve.mark()
                yield
                for j in range(0, hp, 4):
                    nh = min(4, hp)
                    w = nh * P
                    n = len(folded)
                    bank_a, bank_b, bank_c = banks[n % len(banks)]
                    pe.wait(spread_ready)
                    if n >= len(banks):
                        pe.wait(folded[n - len(banks)])
                    rhs = spread[:, j:j + nh, :]
                    mm(ps[:, bank_a, 0:w], wkT[:, i, 0:P], rhs, True, True)
                    mm(ps[:, bank_b, 0:w], wkT[:, i, P:256], rhs, True, True)
                    if bk:
                        mm(ps[0:1, bank_c, 0:w], col(bk, i), rhs, True, True)
                    got = pe.mark()
                    spread_free = got
                    s = slice((i * hp + j) * P, (i * hp + j + nh) * P)
                    act.wait(got)
                    copy(act, q_a_hi[:, s], ps[:, bank_a, 0:w])
                    copy(act, q_b[:, s], ps[:, bank_b, 0:w])
                    hi_ready = act.mark()
                    dve.wait(hi_ready)
                    tt(dve, q_a_lo[:, s], ps[:, bank_a, 0:w], q_a_hi[:, s], ALU.subtract)
                    tt(dve, q_c[0:CB_ROW, s], ps[0:CB_ROW, bank_b, 0:w], q_b[0:CB_ROW, s], ALU.subtract)
                    copy(dve, q_m[0:CB_ROW, s], q_b[0:CB_ROW, s])
                    if bk:
                        chi, clo = (att[0:1, n * 256:(n + 1) * 256].bitcast(F16) for n in range(2))
                        if rows_in:
                            dve.wait(rows_in)
                        copy(dve, chi, ps[0:1, bank_c, 0:w])
                        dve.settle()
                        tt(dve, clo, ps[0:1, bank_c, 0:w], chi, ALU.subtract)
                    done = dve.mark()
                    folded.append(done)
                    if bk:
                        sp.wait(done)
                        for q in (q_c, q_m):
                            for r, part in ((C_ROW, chi), (C_ROW + 1, clo)):
                                rows_in = ld_rows.load(sp, q[r:r + 1, s], part)
                    yield
            pe.wait(*folded)
            if rows_in:
                pe.wait(rows_in)
            L.folded = folded[-1]

        def attend(L, q_free=()):
            mpart = small[:, 64:64 + H * (len(DIRECT) + 1)].rearrange("p (h s) -> p h s", h=H)
            mx = small[:, 192:192 + H]
            BLK = MAXC * MAXB
            p16_flat = p16[:, :, :].rearrange("p a b -> p (a b)")
            copied = [p16_flat[:, n * BLK:(n + 1) * BLK] for n in range(4)]
            running = att[:, :].bitcast(F16)[:, 0:BLK]
            left = [None] * 4
            taken = [L.folded] * 4
            total_copied = 0
            rows_in = []

            def shift_rows(g):
                m = mx[:, 8 * g:8 * g + 8]
                reduce(m, mpart[:, 8 * g:8 * g + 8, :], AX.X, ALU.max).settle()
                ts(dve, m, m, -1.0, EXP_SHIFT, ALU.mult, ALU.add)
                shift_ready = dve.mark()
                n = (8 * g + 8) * NMAX % 4
                pe.wait(shift_ready, left[n])
                for j in range(8):
                    tp(ps[0:1, 2 * n + j // 4, (j % 4) * P:(j % 4 + 1) * P], m[:, j:j + 1], ident[:, :])
                turned = pe.mark()
                hi, lo = (L.rows[:, k * 512:(k + 1) * 512].bitcast(F16) for k in range(2))
                row = ps[0:1, 2 * n:2 * n + 2, :].rearrange("p a b -> p (a b)")
                dve.wait(turned, *rows_in)
                copy(dve, hi, row)
                dve.settle()
                tt(dve, lo, row, hi, ALU.subtract)
                left[n] = dve.mark()
                sp.wait(left[n])
                for k, part in enumerate((hi, lo)):
                    landed = ld_rows.load(sp, q_c[R_ROW + k:R_ROW + k + 1, 1024 * g:1024 * (g + 1)], part)
                return landed

            for h in range(H):
                hs = slice(h * P, (h + 1) * P)
                n_copied, n_direct = 0, 0
                for s in range(NMAX):
                    half = (h * NMAX + s) % 4
                    if left[half]:
                        pe.wait(left[half])
                    for b in range(MAXB):
                        k0 = (s * MAXB + b) * MAXC
                        o = ps[:, half * MAXB + b, 0:MAXC]
                        mm(o, q_a_hi[:, hs], ctxT_a_hi[:, k0:k0 + MAXC], True, False)
                        mm(o, q_m[0:K_C, hs], ctxT_c[0:K_C, k0:k0 + MAXC], False, True)
                    scored = pe.mark()
                    block = ps[:, half * MAXB:(half + 1) * MAXB, 0:MAXC]
                    if s in DIRECT:
                        dve.wait(scored)
                        reduce(mpart[:, h, n_direct:n_direct + 1], block, AX.XY, ALU.max)
                        n_direct += 1
                        left[half] = dve.mark()
                        continue
                    c = total_copied % 4
                    total_copied += 1
                    act.wait(scored, taken[c])
                    copy(act, copied[c].rearrange("p (a b) -> p a b", a=MAXB), block)
                    left[half] = copy_ready = act.mark()
                    n_copied += 1
                    if n_copied == 1:
                        before = c
                        continue
                    dve.wait(copy_ready)
                    if n_copied == 2:
                        tt(dve, running, copied[before], copied[c], ALU.max)
                    else:
                        tt(dve, running, running, copied[c], ALU.max)
                    taken[c] = dve.settle()
                    if n_copied == 2:
                        taken[before] = taken[c]
                w = BLK
                for _ in range(2):
                    w //= 2
                    tt(dve, running[:, 0:w], running[:, 0:w], running[:, w:2 * w], ALU.max)
                    dve.settle()
                reduce(mpart[:, h, n_direct:n_direct + 1], running[:, 0:w], AX.X, ALU.max).settle()
                if h % 8 == 7:
                    rows_in.append(shift_rows(h // 8))
            dh, vw = L.dh, 2 * L.dh + 2
            per_bank = 512 // vw if dh == 64 else 8
            V_BANK, O_BANK = 4, 5
            gw = 8 * dh

            def out_cols(h):
                o = (h % per_bank) * vw
                return ps[:, O_BANK + h // per_bank, o:o + vw]

            sc_free = {}
            unit = 0
            v_free = None
            p_free = [None, None]
            pe.wait(L.wv_ready, *left)
            act.wait(*taken)
            S_BANKS = (0, 1, 2, 3) if L is L1 else (0, 1, 2, 3, 6, 7)
            att_ready = None
            for g in range(2):
                pe.wait(rows_in[g])
                pending = None
                for t in range(NT + 1):
                    if t < NT:
                        b = t % 2
                        ks = slice(t * P, (t + 1) * P)
                        vs = slice(g * gw, (g + 1) * gw)
                        terms = ((ctxT_a_hi[:, ks], q_a_hi, wv16[:, 0, vs]),
                                 (ctxT_a_hi[:, ks], q_a_lo, wv16[:, 1, vs]),
                                 (ctxT_a_lo[:, ks], q_a_hi, wv16[:, 0, vs]),
                                 (ctxT_b[:, ks], q_b, wv16[:, 2, vs]),
                                 (ctxT_c[0:K_C, ks], q_c, wv16[0:CB_ROW, 3, vs]))
                        if v_free:
                            pe.wait(v_free)
                        for n, (key, q, wv) in enumerate(terms):
                            mm(ps[:, V_BANK, 0:gw], key[0:wv.shape[0], :], wv, n == 0, n == len(terms) - 1)
                        valued = pe.mark()
                        v4 = v_tile(L, b)
                        vp = ps[:, V_BANK, 0:gw].rearrange("p (h c) -> p h c", h=8)
                        for j in range(2):
                            bank = S_BANKS[unit % len(S_BANKS)]
                            unit += 1
                            if bank in sc_free:
                                pe.wait(sc_free[bank])
                            for n, (key, q, wv) in enumerate(terms):
                                rhs = q[0:key.shape[0], g * 1024 + j * 512:g * 1024 + (j + 1) * 512]
                                mm(ps[:, bank, :], key, rhs, n == 0, n == len(terms) - 1)
                            scored = pe.mark()
                            phi, plo = (p16[:, k + b, j * 512:(j + 1) * 512] for k in (0, 2))
                            act.wait(scored)
                            if p_free[b]:
                                act.wait(p_free[b])
                            exp(phi, ps[:, bank, :])
                            exp(ps[:, bank, :], ps[:, bank, :])
                            exped = act.mark()
                            if j == 0:
                                dve.wait(valued)
                                if p_free[b]:
                                    dve.wait(p_free[b])
                                copy(dve, v4[:, :, 0:dh], vp)
                                dve.settle()
                                tt(dve, v4[:, :, dh + 2:vw], vp, v4[:, :, 0:dh], ALU.subtract)
                                v_free = dve.mark()
                            dve.wait(exped)
                            tt(dve, plo, ps[:, bank, :], phi, ALU.subtract)
                            sc_free[bank] = low = dve.mark()
                    if pending is not None:
                        pb, pready, pt = pending
                        pe.wait(*pready)
                        if pt == 0 and att_ready:
                            pe.wait(att_ready)
                        v4 = v_tile(L, pb)
                        for h in range(8):
                            o = out_cols(h)
                            first = pt == 0 and h % per_bank == 0
                            kw = dict(skip_group_check=True)
                            hh = slice(h * P, (h + 1) * P)
                            mm(o, p16[:, pb, hh], v4[:, h, :], first, False, **kw)
                            mm(o[:, 0:dh + 2], p16[:, 2 + pb, hh], v4[:, h, 0:dh + 2], False, pt == NT - 1, **kw)
                        p_free[pb] = pe.mark()
                    pending = (b, (exped, v_free, low), t) if t < NT else None
                summed = p_free[(NT - 1) % 2]
                inv = small[:, 224:232]
                dve.wait(summed)
                for h0 in range(0, 8, per_bank):
                    nh = min(per_bank, 8 - h0)
                    o = ps[:, O_BANK + h0 // per_bank, 0:nh * vw].rearrange("p (h c) -> p h c", h=nh)
                    a = att[:, g * gw + h0 * dh:g * gw + (h0 + nh) * dh].rearrange("p (h c) -> p h c", h=nh)
                    i = inv[:, h0:h0 + nh]
                    ts(dve, i, o[:, :, dh], VS, None, ALU.mult)
                    copy(dve, a, o[:, :, 0:dh])
                    dve.settle()
                    reciprocal(i, i)
                    tt(dve, a, o[:, :, dh + 2:vw], a, ALU.add)
                    dve.settle()
                    tt(dve, a, a, bc(i, 2, [P, nh, dh]), ALU.mult)
                att_ready = dve.settle()
            return (att_ready,)

        split_chunk(0)
        xnT_ready = layernorm((x_in,), 5)
        steps = fold_queries(L0, l0_proj_in, "L0_xattn_bq", "L0_xattn_bk", xnT_ready, ((5, 6, 7),))
        for c in range(NCH):
            if c + 1 < NCH:
                split_chunk(c + 1)
            if c == 1:
                load_split(ld_w2, L0.wv, d["L0_xattn_Wv"])
                load_blocks(ld_w2, W[:, W1_OFF:], d["L0_xattn_W1"])
                load_blocks(ld_w2, W[:, W2_OFF:], d["L0_xattn_W2"])
                l0_rest_in = load_blocks(ld_w2, W[:, CA_OFF:], d["L0_attn_c_attn_w"])
            turn_chunk(c)
            next(steps, None)
        for _ in steps:
            pass
        L0.wv_ready = split_wv(L0, l0_rest_in)

        EXPERT0 = (stage[:, 0:4096], W[:, 5632:9728], W[:, 0:4096])

        def load_expert0(e, *free):
            region = EXPERT0[e % 3]
            sp.wait(*free)
            load_blocks(ld_exp[e % 3], region[:, 0:2048], d["L0_ffn_W1"][e])
            return load_blocks(ld_exp[e % 3], region[:, 2048:4096], d["L0_ffn_W2"][e])

        chunks_read = (halves[NCH - 1], halves[NCH - 2], halves[NCH - 3], read_done[0], read_done[1])
        sp.wait(*chunks_read)
        dve.wait(*chunks_read)
        clear(bias_rows, 0.0)
        sp.wait(dve.settle())
        BR = {}
        for n, (name, lo_, w) in enumerate((("L0_xattn_b2", 0, D), ("L0_attn_c_attn_b", 2 * D, D),
                                            ("L0_attn_c_proj_b", 0, D), ("L1_xattn_bo", 0, D),
                                            ("L0_ffn_bg", 0, NE))):
            BR[name] = n
            ld_bias.load(sp, bias_rows[n:n + 1, 0:w],
                         d[name].rearrange("(a n) -> a n", a=1)[:, lo_:lo_ + w])
        load_blocks(ld_bias, tail[:, 272:784], d["L0_attn_c_proj_w"])
        load_blocks(ld_bias, tail[:, 256:272], d["L0_ffn_Wg"])
        tail_in = ld_bias.load(sp, bias2, d["L0_ffn_b2"])
        loaded = [load_expert0(0), load_expert0(1)]
        pe.wait(*evac[NCH - 2], *evac[NCH - 1])
        att_ready = attend(L0)

        attT = scratch[:, 0:2 * P].rearrange("p (a q) -> p a q", a=2)
        hT = scratch[:, 256:256 + 4 * P].rearrange("p (a q) -> p a q", a=4)
        pe.wait(*att_ready)
        pe.wait(tail_in)
        for i in range(2):
            tp(ps[:, 0, i * P:(i + 1) * P], att[:, i * P:(i + 1) * P], ident[:, :])
        turned = pe.mark()
        dve.wait(turned)
        for i in range(2):
            ts(dve, attT[:, i, :], ps[:, 0, i * P:(i + 1) * P], col("L0_xattn_bv", i), None, ALU.add)
        ready = dve.mark()
        pe.wait(ready)
        w1, w2 = wview(W1_OFF, 2, 512), wview(W2_OFF, 4, D)
        for f in range(4):
            for a in range(2):
                mm(ps[:, 1, f * P:(f + 1) * P], w1[:, a, f * P:(f + 1) * P], attT[:, a, :], a == 0, a == 1)
        ready = pe.mark()
        dve.wait(ready)
        for f in range(4):
            ts(dve, hT[:, f, :], ps[:, 1, f * P:(f + 1) * P], col("L0_xattn_b1", f), 0.0, ALU.add, ALU.max)
        ready = dve.mark()
        pe.wait(ready)
        for f in range(4):
            mm(ps[:, 2, 0:D], hT[:, f, :], w2[:, f, :], f == 0, False)
        mm(ps[:, 2, 0:D], row_select(BR["L0_xattn_b2"]), bias_rows, False, True)
        x_ready = residual(ps[:, 2, 0:D], pe.mark())
        loaded.append(load_expert0(2, x_ready))

        xnT_ready = layernorm(())
        ca = wview(CA_OFF, 2, 3 * D)
        qkT = scratch[:, 0:512].rearrange("p (a q) -> p a q", a=4)
        v_tok = scratch[:, 512:768]
        spread = scratch[:, 768:768 + 2048].rearrange("p (h q) -> p h q", h=H)
        probT = scratch[:, 768:768 + 2048].rearrange("p (h q) -> p h q", h=H)
        prob = scratch[:, 2816:2816 + 2048].rearrange("p (h q) -> p h q", h=H)
        pe.wait(xnT_ready)
        for n in range(4):
            for a in range(2):
                mm(ps[:, 1, n * P:(n + 1) * P], ca[:, a, n * P:(n + 1) * P], xnT[:, a, :], a == 0, a == 1)
        qk_in = pe.mark()
        for a in range(2):
            mm(ps[:, 2, 0:D], xnT[:, a, :], ca[:, a, 2 * D:3 * D], a == 0, False)
        mm(ps[:, 2, 0:D], row_select(BR["L0_attn_c_attn_b"]), bias_rows, False, True)
        v_in = pe.mark()
        dve.wait(qk_in)
        for n in range(4):
            ts(dve, qkT[:, n, :], ps[:, 1, n * P:(n + 1) * P], col("L0_attn_c_attn_b", n),
               0.25 if n < 2 else 1.0, ALU.add, ALU.mult)
        dve.settle()
        for i in range(2):
            tt(dve, spread[:, 8 * i:8 * i + 8, :], bc(qkT[:, i, :], 1, [P, 8, P]),
               bc(head16[:, :], 2, [P, 8, P]), ALU.mult)
        spread_ready = dve.mark()
        act.wait(v_in)
        copy(act, v_tok, ps[:, 2, 0:D])
        v_ready = act.mark()
        pe.wait(spread_ready)
        sc = ps[:, 4:8, :]
        for b in range(4):
            mm(ps[:, 4 + b, :], ident[:, :], bc(causal[:, :], 1, [P, 4, P]), True, False, skip_group_check=True)
            for j in range(4):
                h = 4 * b + j
                mm(ps[:, 4 + b, j * P:(j + 1) * P], spread[:, h, :], qkT[:, 2 + h // 8, :], False, True,
                   skip_group_check=True)
        scored = pe.mark()
        mx, tot = small[:, 16:32], small[:, 32:48]
        sch = sc.rearrange("p b (j q) -> p b j q", j=4)

        def by4(t):
            return t.rearrange("p (b j) -> p b j", b=4)

        dve.wait(scored)
        reduce(by4(mx), sch, AX.X, ALU.max).settle()
        tt(dve, prob.rearrange("p (b j) q -> p b j q", b=4), sch, bc(by4(mx), 3, [P, 4, 4, P]), ALU.subtract)
        centred = dve.mark()
        act.wait(centred)
        exp(prob, prob)
        exped = act.mark()
        dve.wait(exped)
        reduce(tot, prob, AX.X, ALU.add).settle()
        reciprocal(tot, tot).settle()
        pe.wait(exped)
        for h in range(H):
            tp(ps[:, h // 4, (h % 4) * P:(h % 4 + 1) * P], prob[:, h, :], ident[:, :])
        turned = pe.mark()
        act.wait(turned)
        copy(act, probT[:, 0:8, :].rearrange("p (b j) q -> p b (j q)", b=2), ps[:, 0:2, :])
        t1 = act.mark()
        dve.wait(turned)
        copy(dve, probT[:, 8:16, :].rearrange("p (b j) q -> p b (j q)", b=2), ps[:, 2:4, :])
        t2 = dve.mark()
        pe.wait(t1, t2, v_ready)
        for h in range(H):
            mm(ps[:, 4, h * 16:(h + 1) * 16], probT[:, h, :], v_tok[:, h * 16:(h + 1) * 16], True, True)
        ready = pe.mark()
        dve.wait(ready)
        tt(dve, att[:, 0:D].rearrange("p (h d) -> p h d", h=H), ps[:, 4, 0:D].rearrange("p (h d) -> p h d", h=H),
           bc(tot, 2, [P, H, 16]), ALU.mult)
        ready = dve.mark()
        attT_ready = transpose_act(att, 2, attT, (ready,), 5)
        pe.wait(attT_ready)
        for a in range(2):
            mm(ps[:, 6, 0:D], attT[:, a, :], cp[:, a, :], a == 0, False)
        mm(ps[:, 6, 0:D], row_select(BR["L0_attn_c_proj_b"]), bias_rows, False, True)
        x_ready = residual(ps[:, 6, 0:D], pe.mark())

        def gate(logits, ready, second_softmax):
            pr, w, mxe, tot = small[:, 240:248], small[:, 248:256], small[:, 256:257], small[:, 257:258]
            rank = small[:, 264:272]
            grid, eq = small[:, 272:336], small[:, 336:400]
            g3, q3 = (t.rearrange("p (e j) -> p e j", e=NE) for t in (grid, eq))
            dve.wait(ready)
            reduce(mxe, logits, AX.X, ALU.max).settle()
            ts(dve, pr, logits, mxe, None, ALU.subtract)
            t = dve.mark()
            act.wait(t)
            exp(pr, pr)
            t = act.mark()
            dve.wait(t)
            reduce(tot, pr, AX.X, ALU.add).settle()
            reciprocal(tot, tot).settle()
            ts(dve, pr, pr, tot, None, ALU.mult)
            dve.settle()
            pj, pe_ = bc(pr, 1, [P, NE, NE]), bc(pr, 2, [P, NE, NE])
            tt(dve, g3, pj, pe_, ALU.is_gt)
            tt(dve, q3, pj, pe_, ALU.is_equal)
            dve.settle()
            tt(dve, q3, q3, lower[:, :, :], ALU.mult)
            dve.settle()
            tt(dve, g3, g3, q3, ALU.add)
            dve.settle()
            reduce(rank, g3, AX.X, ALU.add).settle()
            ts(dve, rank, rank, 1.5, None, ALU.is_lt)
            if second_softmax:
                reduce(mxe, pr, AX.X, ALU.max).settle()
                ts(dve, pr, pr, mxe, None, ALU.subtract)
                t = dve.mark()
                act.wait(t)
                exp(pr, pr)
                t = act.mark()
                dve.wait(t)
            else:
                dve.settle()
            tt(dve, w, pr, rank, ALU.mult)
            dve.settle()
            reduce(tot, w, AX.X, ALU.add).settle()
            if not second_softmax:
                ts(dve, tot, tot, 1e-6, None, ALU.add)
                dve.settle()
            reciprocal(tot, tot).settle()
            ts(dve, w, w, tot, None, ALU.mult)
            dve.settle()
            return w

        xnT_ready = layernorm(())
        pe.wait(xnT_ready)
        for a in range(2):
            mm(ps[:, 1, 0:NE], xnT[:, a, :], wg[:, a, :], a == 0, False)
        mm(ps[:, 1, 0:NE], row_select(BR["L0_ffn_bg"]), bias_rows[:, 0:NE], False, True)
        w_e = gate(ps[:, 1, 0:NE], pe.mark(), False)
        w_ready = dve.mark() if dve.steps[-1][1] is None else (dve.sem, dve.count)
        wT = scratch[0:8, 4480:4480 + P]
        pe.wait(w_ready)
        tp(ps[0:8, 2, 0:P], w_e, ident[:, :])
        t = pe.mark()
        act.wait(t)
        copy(act, wT, ps[0:8, 2, 0:P])
        t = act.mark()
        pe.wait(t)
        mm(ps[:, 1, 0:D], wT, bias2, True, True)
        residual(ps[:, 1, 0:D], pe.mark())
        NF = F0 // P
        hT2 = [scratch[:, 2048 * 0 + 1024 * n:1024 * (n + 1)].rearrange("p (f q) -> p f q", f=NF) for n in range(2)]
        h_free, y_free, hidden = [None, None], [None, None], [None, None]

        def hidden0(e_):
            b = e_ % 2
            w1 = by_rows(EXPERT0[e_ % 3][:, 0:2048], 2, F0)
            pe.wait(loaded[e_])
            if hidden[b]:
                pe.wait(hidden[b])
            for k in range(NF // 4):
                bank = 2 + 2 * b + k
                for j in range(4):
                    f = 4 * k + j
                    for a in range(2):
                        mm(ps[:, bank, j * P:(j + 1) * P], w1[:, a, f * P:(f + 1) * P], xnT[:, a, :], a == 0, a == 1)
                summed = pe.mark()
                act.wait(summed)
                if h_free[b]:
                    act.wait(h_free[b])
                for j in range(4):
                    gelu(hT2[b][:, 4 * k + j, :], ps[:, bank, j * P:(j + 1) * P], col("L0_ffn_b1", e_ * NF + 4 * k + j))
            hidden[b] = act.mark()

        def down0(e_):
            b = e_ % 2
            w2 = by_rows(EXPERT0[e_ % 3][:, 2048:4096], NF, D)
            pe.wait(hidden[b])
            if y_free[b]:
                pe.wait(y_free[b])
            for f in range(NF):
                mm(ps[:, 6 + b, 0:D], hT2[b][:, f, :], w2[:, f, :], f == 0, f == NF - 1)
            y = pe.mark()
            h_free[b] = y
            dve.wait(y)
            weigh(ps[:, 6 + b, 0:D], w_e[:, e_:e_ + 1])
            y_free[b] = dve.settle()

        for e_ in range(NE + 1):
            if e_ < NE:
                hidden0(e_)
            if e_:
                down0(e_ - 1)
                done = h_free[(e_ - 1) % 2]
                if e_ + 2 < NE:
                    loaded.append(load_expert0(e_ + 2, done))
                elif e_ + 2 == NE:
                    sp.wait(done)
                    load_blocks(ld_w, L1.wq, d["L1_xattn_Wq"])
                    l1_proj_in = load_split(ld_w, L1.wk, d["L1_xattn_Wk"])
                elif e_ + 1 == NE:
                    sp.wait(done)
                    load_split(ld_w2, L1.wv, d["L1_xattn_Wv"])
                    l1_wv_in = load_blocks(ld_w2, L1.wo, d["L1_xattn_Wo"])
        x_ready = y_free[(NE - 1) % 2]

        xnT_ready = layernorm(())
        dve.do(lambda e: e.memset(q_c[CB_ROW:P, :], 0.0))
        dve.do(lambda e: e.memset(q_m[CB_ROW:P, :], 0.0)).settle()
        act.wait((dve.sem, dve.count))
        for _ in fold_queries(L1, l1_proj_in, None, None, xnT_ready, ((2, 3, 4), (5, 6, 7))):
            pass
        L1.wv_ready = split_wv(L1, l1_wv_in)

        EXPERT1 = (W[:, 0:3072], W[:, 3072:6144], W[:, 6656:9728])
        wa, wr = by_rows(W[:, 6144:6656], 2, D), by_rows(W[:, 9728:], 2, NE)

        def load_expert1(e, *free):
            region = EXPERT1[e % 3]
            sp.wait(*free)
            load_blocks(ld_exp[e % 3], region[:, 0:1024], d["L1_ffn_kernel_gating_EDF"][e])
            load_blocks(ld_exp[e % 3], region[:, 1024:2048], d["L1_ffn_kernel_up_EDF"][e])
            return load_blocks(ld_exp[e % 3], region[:, 2048:3072], d["L1_ffn_kernel_down_EFD"][e])

        sp.wait(L1.folded)
        load_blocks(ld_bias, W[:, 6144:6656], d["L1_attn_W"])
        gate_in = load_blocks(ld_bias, W[:, 9728:], d["L1_ffn_router_kernel_DE"])
        loaded = [load_expert1(e, L1.folded) for e in range(3)]
        att_ready = attend(L1)
        attT = scratch[:, 0:1024].rearrange("p (a q) -> p a q", a=8)
        attT_ready = transpose_act(att, 8, attT, att_ready, 1)
        wo = by_rows(L1.wo, 8, D)
        pe.wait(attT_ready)
        for a in range(8):
            mm(ps[:, 3, 0:D], attT[:, a, :], wo[:, a, :], a == 0, False)
        mm(ps[:, 3, 0:D], row_select(BR["L1_xattn_bo"]), bias_rows, False, True)
        x_ready = residual(ps[:, 3, 0:D], pe.mark())

        NF1 = F1 // P

        xnT_ready = layernorm(())
        prob, mask = scratch[:, 0:128], scratch[:, 128:256]
        mx, tot, vac, spr = small[:, 16:17], small[:, 17:18], small[:, 18:19], small[:, 19:20]
        wsum = small[:, 20:22]
        pe.wait(xnT_ready)
        for a in range(2):
            mm(ps[:, 1, 0:P], xnT[:, a, :], xnT[:, a, :], a == 0, a == 1)
        scored = pe.mark()
        dve.wait(scored, x_ready)
        reduce(mx, ps[:, 1, 0:P], AX.X, ALU.max).settle()
        ts(dve, prob, ps[:, 1, 0:P], mx, 1.0 / 16, ALU.subtract, ALU.mult)
        t = dve.mark()
        act.wait(t)
        exp(prob, prob)
        t = act.mark()
        dve.wait(t)
        reduce(tot, prob, AX.X, ALU.add).settle()
        reciprocal(tot, tot).settle()
        ts(dve, prob, prob, tot, None, ALU.mult)
        dve.settle()
        ts(dve, mask, prob, 0.01, None, ALU.is_lt)
        dve.settle()
        tt(dve, mask, mask, prob, ALU.mult)
        dve.settle()
        reduce(vac, mask, AX.X, ALU.add)
        tt(dve, prob, prob, mask, ALU.subtract)
        dve.settle()
        reduce(spr, prob, AX.X, ALU.add).settle()
        ts(dve, spr, spr, 1e-9, None, ALU.add)
        dve.settle()
        reciprocal(spr, spr).settle()
        ts(dve, prob, prob, spr, None, ALU.mult)
        dve.wait(gate_in)
        reduce(wsum, wa, AX.X, ALU.add).settle()
        ts(dve, wsum, wsum, 0.01, None, ALU.mult)
        t = dve.mark()
        pe.wait(t)
        tp(ps[:, 2, 0:P], prob, ident[:, :])
        tp(ps[0:1, 2, P:2 * P], vac, ident[:, :])
        for a in range(2):
            tp(ps[0:1, 2, (2 + a) * P:(3 + a) * P], wsum[:, a:a + 1], ident[:, :])
        t = pe.mark()
        act.wait(t)
        probT = scratch[:, 256:384]
        rows = scratch[0:1, 384:384 + 384]
        copy(act, probT, ps[:, 2, 0:P])
        copy(act, rows, ps[0:1, 2, P:4 * P])
        t = act.mark()
        pe.wait(t)
        mm(ps[:, 3, 0:D], probT, xn[:, :], True, False)
        mm(ps[:, 3, 0:D], rows[:, 0:P], rows[:, P:3 * P], False, True)
        x_ready = residual(ps[:, 3, 0:D], pe.mark())

        xnT_ready = layernorm(())
        pe.wait(xnT_ready, gate_in)
        for a in range(2):
            mm(ps[:, 1, 0:NE], xnT[:, a, :], wr[:, a, :], a == 0, a == 1)
        w_e = gate(ps[:, 1, 0:NE], pe.mark(), True)
        fuse = [scratch[:, 1024 * n:1024 * n + NF1 * P].rearrange("p (f q) -> p f q", f=NF1) for n in range(2)]
        sig = [scratch[:, 1024 * n + 512:1024 * n + 512 + NF1 * P] for n in range(2)]
        h_free, y_free, fused = [None, None], [None, None], [None, None]

        def hidden1(e_):
            b = e_ % 2
            region = EXPERT1[e_ % 3]
            wgt, wup = by_rows(region[:, 0:1024], 2, F1), by_rows(region[:, 1024:2048], 2, F1)
            gp, up = ps[:, 2 + 2 * b, :], ps[:, 3 + 2 * b, :]
            pe.wait(loaded[e_])
            if fused[b]:
                pe.wait(fused[b])
            made = []
            for o, w in ((gp, wgt), (up, wup)):
                for f in range(NF1):
                    for a in range(2):
                        mm(o[:, f * P:(f + 1) * P], w[:, a, f * P:(f + 1) * P], xnT[:, a, :], a == 0, a == 1)
                made.append(pe.mark())
            act.wait(made[0])
            if fused[b]:
                act.wait(fused[b])
            exp(sig[b], gp, scale=-1.0)
            exped = act.mark()
            dve.wait(exped)
            ts(dve, sig[b], sig[b], 1.0, None, ALU.add)
            dve.settle()
            reciprocal(sig[b], sig[b]).settle()
            tt(dve, sig[b], gp, sig[b], ALU.mult)
            dve.settle()
            dve.wait(made[1])
            if h_free[b]:
                dve.wait(h_free[b])
            tt(dve, fuse[b].rearrange("p f q -> p (f q)"), up, sig[b], ALU.mult)
            fused[b] = dve.mark()

        def down1(e_):
            b = e_ % 2
            wdn = by_rows(EXPERT1[e_ % 3][:, 2048:3072], NF1, D)
            pe.wait(fused[b])
            if y_free[b]:
                pe.wait(y_free[b])
            for f in range(NF1):
                mm(ps[:, 6 + b, 0:D], fuse[b][:, f, :], wdn[:, f, :], f == 0, f == NF1 - 1)
            y = pe.mark()
            h_free[b] = y
            dve.wait(y)
            weigh(ps[:, 6 + b, 0:D], w_e[:, e_:e_ + 1])
            y_free[b] = dve.settle()

        for e_ in range(NE + 1):
            if e_ < NE:
                hidden1(e_)
            if e_:
                down1(e_ - 1)
                if e_ + 2 < NE:
                    loaded.append(load_expert1(e_ + 2, h_free[(e_ - 1) % 2]))
        sp.wait(y_free[(NE - 1) % 2])
        sp.wait(st_out.load(sp, out[0], x[:, :]))

        block = ctx.enter_context(nc.Block())
        block.tensor(pe.run)
        block.scalar(act.run)
        block.vector(dve.run)
        block.gpsimd(pool.run)
        block.sync(sp.run)


_OUTS = [((1, 128, 256), "float32")]


def kernel(**inputs):
    import numpy as _np
    import concourse.bacc as _bacc
    from concourse import mybir as _mybir
    from concourse.bass_utils import run_bass_kernel_spmd as _run

    nc = _bacc.Bacc("TRN2", target_bir_lowering=False, num_devices=1)
    arrays, args = {}, {}
    for name in inputs:
        a = _np.ascontiguousarray(inputs[name])
        arrays[f"in_{name}_dram"] = a
        args[name] = nc.dram_tensor(f"in_{name}_dram", a.shape, _mybir.dt.from_np(a.dtype), kind="ExternalInput").ap()
    shape, dtype = _OUTS[0]
    out = nc.dram_tensor("out_0_dram", shape, _mybir.dt.from_np(_np.dtype(dtype)), kind="ExternalOutput").ap()
    perceiver_kernel(nc, args, out)
    r = _run(nc, [arrays], core_ids=[0])
    return r.results[0]["out_0_dram"]
```

```python
from contextlib import ExitStack

import numpy as np

import concourse.bass as bass
from concourse import mybir

F32 = mybir.dt.float32
F16 = mybir.dt.float16
ALU = mybir.AluOpType
ACT = mybir.ActivationFunctionType
AX = mybir.AxisListType

P = 128
EPS = 1e-5
EXP_SHIFT = 8 * 0.6931471805599453
ONES16 = float(np.array([0x3C003C00], np.uint32).view(np.float32)[0])


class Queue:

    def __init__(self, sem):
        self.sem, self.count, self.steps, self.known = sem, 0, [], {}

    def do(self, build):
        self.steps.append([build, None])
        return self

    def mark(self):
        assert self.steps[-1][1] is None
        self.count += 1
        self.steps[-1][1] = self.sem
        return (self.sem, self.count)

    def wait(self, *tokens):
        for sem, value in tokens:
            if self.known.get(sem.name, 0) < value:
                self.known[sem.name] = value
                self.steps.append([lambda e, s=sem, v=value: e.wait_ge(s, v), "wait"])
        return self

    def settle(self):
        token = self.mark()
        self.wait(token)
        return token

    def run(self, engine):
        for build, sem in self.steps:
            ins = build(engine)
            if sem is not None and sem != "wait":
                ins.then_inc(sem, 1)


class Landing:

    def __init__(self, sem):
        self.sem, self.total = sem, 0

    def load(self, queue, out, in_):
        self.total += 16
        queue.steps.append([lambda e, o=out, i=in_, s=self.sem: e.dma_start(o, i).then_inc(s, 16), "wait"])
        return (self.sem, self.total)


def perceiver_kernel(nc, d, out):
    _, N_TOK, D = d["x"].shape
    _, M, C = d["ctx_768"].shape
    H = 16
    NE = d["L0_ffn_Wg"].shape[1]
    F0 = d["L0_ffn_W1"].shape[2]
    F1 = d["L1_ffn_kernel_gating_EDF"].shape[2]
    assert N_TOK == P and D == 2 * P and C == 192 and M % P == 0
    NT = M // P
    CH = 7
    NCH = NT // CH
    assert NT % CH == 0
    CW = CH * C
    VS = 32.0
    MAXC = 448
    MAXB = 2
    NMAX = M // (MAXC * MAXB)
    assert NMAX * MAXC * MAXB == M
    DIRECT = (2, 5, 8, 11)
    CB_ROW = C - P
    HI_ROW, LO_ROW, K_C = 64, 96, 97

    ctx = ExitStack()
    with ctx:
        def sb(name, shape, dt):
            return ctx.enter_context(nc.sbuf_tensor(name, shape, dt))

        def sem(name):
            return ctx.enter_context(nc.semaphore(name))

        ctxT_a_hi = sb("ctxT_a_hi", [P, M], F16)
        ctxT_a_lo = sb("ctxT_a_lo", [P, M], F16)
        ctxT_b = sb("ctxT_b", [P, M], F16)
        ctxT_c = sb("ctxT_c", [P, M], F16)
        q_all = sb("q_all", [P, 5, H * P], F16)
        q_a_hi, q_a_lo, q_b, q_c, q_m = (q_all[:, n, :] for n in range(5))
        q_s = q_a_lo
        keys = q_b.rearrange("p (n b j k) -> p n b j k", n=2, b=2, j=2)
        k_both, k_hi = keys[:, 0], keys[:, 1]
        scratch = q_all[:, :, :].rearrange("p a b -> p (a b)").bitcast(F32)
        p16 = sb("p16", [P, 4, 8 * P], F16)
        stage = sb("stage", [P, 4 * CW], F32)
        ctx16 = [stage[:, n * CW:(n + 1) * CW].bitcast(F16).rearrange("p (t c) -> p t c", t=CH)
                 for n in range(4)]
        tail = stage[:, 4096:4 * CW]
        bias2 = tail[0:8, 0:D]
        wg = tail[:, 256:272].rearrange("p (a n) -> p a n", a=2)
        bias_rows = tail[0:8, 784:784 + D]
        wv16 = sb("wv16", [P, 4, 1024], F16)
        v16 = sb("v16", [P, 2 * 8 * 130], F16)
        W = sb("W", [P, 9744], F32)
        ctx32 = [W[:, 5632 + n * CW:5632 + (n + 1) * CW] for n in range(3)]
        x = sb("x_tok", [P, D], F32)
        xn = sb("xn", [P, D], F32)
        xnT = sb("xnT", [P, 2, P], F32)
        att = sb("att", [P, 1024], F32)
        ident = sb("ident", [P, P], F32)
        ident16 = sb("ident16", [P, P], F16)
        causal = sb("causal", [P, P], F32)
        head16 = sb("head16", [P, 8], F32)
        head64 = sb("head64", [P, 2], F32)
        lower = sb("lower", [P, NE, NE], F32)
        cols = sb("cols", [P, P], F32)
        small = sb("small", [P, 400], F32)
        minus_half = sb("minus_half", [P, 1], F32)
        ps = ctx.enter_context(nc.psum_tensor("ps", [P, 8, 512], F32))

        def row_select(n):
            return ident[0:8, n:n + 1].to_broadcast([8, P])

        pe, act, dve, pool, sp = (Queue(sem(f"{n}_done")) for n in ("pe", "act", "dve", "pool", "sp"))
        ld_x = Landing(sem("ld_x"))
        ld_bias = Landing(sem("ld_bias"))
        ld_w = Landing(sem("ld_w"))
        ld_w2 = Landing(sem("ld_w2"))
        ld_exp = [Landing(sem(f"ld_exp{n}")) for n in range(3)]
        ld_ctx = [Landing(sem(f"ld_ctx{n}")) for n in range(3)]
        st_out = Landing(sem("st_out"))

        def mm(out, lhsT, rhs, start, stop, **kw):
            pe.do(lambda e: e.matmul(out, lhsT, rhs, start=start, stop=stop, **kw))

        def tp(out, in_, idt):
            pe.do(lambda e: e.transpose(out, in_, idt))

        def copy(q, out, in_):
            if q is act:
                q.do(lambda e: e.copy(out, in_))
            else:
                q.do(lambda e: e.tensor_copy(out, in_))

        def tt(q, out, a, b, op):
            q.do(lambda e: e.tensor_tensor(out, a, b, op))

        def ts(q, out, a, s1, s2, op0, op1=None):
            if op1 is None:
                q.do(lambda e: e.tensor_scalar(out, a, s1, None, op0))
            else:
                q.do(lambda e: e.tensor_scalar(out, a, s1, s2, op0, op1))

        def reduce(out, in_, axis, op):
            return dve.do(lambda e: e.tensor_reduce(out, in_, axis, op))

        def reciprocal(out, in_):
            return dve.do(lambda e: e.reciprocal(out, in_))

        def exp(out, in_, scale=1.0):
            act.do(lambda e: e.activation(out, in_, ACT.Exp, scale=scale))

        def low_part(out, whole, bias, hi):
            dve.do(lambda e: e.scalar_tensor_tensor(out=out, in0=whole, scalar=bias, in1=hi,
                                                    op0=ALU.add, op1=ALU.subtract))

        def add_bias(out, in_, bias):
            act.do(lambda e: e.activation(out, in_, ACT.Identity, bias=bias))

        def clear(q, out, value):
            q.do(lambda e: e.memset(out, value))

        def gelu(out, in_, bias):
            act.do(lambda e: e.activation(out, in_, ACT.Gelu_apprx_tanh, bias=bias))

        def silu(out, in_):
            act.do(lambda e: e.activation(out, in_, ACT.Silu))

        def weigh(y, w):
            dve.do(lambda e: e.scalar_tensor_tensor(out=x[:, :], in0=y, scalar=w, in1=x[:, :],
                                                    op0=ALU.mult, op1=ALU.add))

        def bc(ap, axis, shape):
            return ap.unsqueeze(axis).to_broadcast(shape)

        def layernorm(ready, bank=0):
            stats, mv, rstd = small[:, 0:6], small[:, 6:8], small[:, 8:9]
            dve.wait(*ready)
            dve.do(lambda e: e.bn_stats(stats, x[:, :])).settle()
            dve.do(lambda e: e.bn_aggr(mv, stats)).settle()
            ts(dve, rstd, mv[:, 1:2], EPS, None, ALU.add)
            var_ready = dve.mark()
            pool.wait(var_ready)
            tt(pool, rstd, rstd, minus_half[:, :], ALU.pow)
            rstd_ready = pool.mark()
            dve.wait(rstd_ready)
            ts(dve, xn[:, :], x[:, :], mv[:, 0:1], rstd, ALU.subtract, ALU.mult)
            xn_ready = dve.mark()
            pe.wait(xn_ready)
            for i in range(2):
                tp(ps[:, bank, i * P:(i + 1) * P], xn[:, i * P:(i + 1) * P], ident[:, :])
            turned = pe.mark()
            act.wait(turned)
            copy(act, xnT[:, :, :], ps[:, bank, 0:2 * P].rearrange("p (a b) -> p a b", a=2))
            return act.mark()

        def residual(y, ready):
            dve.wait(ready)
            tt(dve, x[:, :], y, x[:, :], ALU.add)
            return dve.settle()

        def transpose_act(src, n, dst, ready, bank):
            pe.wait(*ready)
            for i in range(n):
                tp(ps[:, bank + i // 4, (i % 4) * P:(i % 4 + 1) * P], src[:, i * P:(i + 1) * P], ident[:, :])
            turned = pe.mark()
            act.wait(turned)
            nb = -(-n // 4)
            w = min(n, 4) * P
            copy(act, dst.rearrange("p (b i) q -> p b (i q)", b=nb), ps[:, bank:bank + nb, 0:w])
            return act.mark()

        pool.do(lambda e: e.memset(ident[:, :], 0.0))
        pool.do(lambda e: e.memset(causal[:, :], 0.0))
        pool.do(lambda e: e.memset(minus_half[:, :], -0.5))
        pool.do(lambda e: e.memset(head16[:, :], 1.0))
        pool.do(lambda e: e.memset(head64[:, :], 1.0))
        pool.do(lambda e: e.memset(lower[:, :, :], 1.0)).settle()
        pool.do(lambda e: e.affine_select(out=ident[:, :], in_=ident[:, :], compare_op=ALU.not_equal,
                                          fill=1.0, base=0, pattern=[[-1, P]], channel_multiplier=1))
        pool.do(lambda e: e.affine_select(out=causal[:, :], in_=causal[:, :], compare_op=ALU.is_ge,
                                          fill=-1e10, base=0, pattern=[[-1, P]], channel_multiplier=1))
        for t, n, w in ((head16, 8, 16), (head64, 2, 64)):
            pool.do(lambda e, t=t, n=n, w=w: e.affine_select(
                out=t[:, :], in_=t[:, :], compare_op=ALU.is_ge, fill=0.0, base=0,
                pattern=[[-w, n]], channel_multiplier=1))
        pool.settle()
        for t, n, w in ((head16, 8, 16), (head64, 2, 64)):
            pool.do(lambda e, t=t, n=n, w=w: e.affine_select(
                out=t[:, :], in_=t[:, :], compare_op=ALU.is_ge, fill=0.0, base=w - 1,
                pattern=[[w, n]], channel_multiplier=-1))
        pool.do(lambda e: e.affine_select(out=lower[:, :, :], in_=lower[:, :, :], compare_op=ALU.is_ge,
                                          fill=0.0, base=-1, pattern=[[1, NE], [-1, NE]],
                                          channel_multiplier=0))
        constants = pool.settle()
        for t in (q_c, q_m):
            pool.do(lambda e, t=t: e.memset(t[CB_ROW:P, :].bitcast(F32), 0.0))
        pool.do(lambda e: e.memset(ctxT_c[CB_ROW:P, :].bitcast(F32), ONES16))
        clear(pool, k_hi[CB_ROW:P], VS)
        rows_blank = pool.settle()
        col_in = att[:, 0:P]
        dve.do(lambda e: e.memset(col_in, 0.0))
        blank = dve.mark()
        dve.wait(constants)
        copy(dve, ident16[:, :], ident[:, :])
        ident16_ready = dve.mark()

        def wview(off, a, b):
            return W[:, off:off + a * b].rearrange("p (a b) -> p a b", a=a)

        def by_rows(region, a, n):
            return region[:, 0:a * n].rearrange("p (a n) -> p a n", a=a)

        def load_blocks(landing, region, src):
            a, n = src.shape[0] // P, src.shape[1]
            return landing.load(sp, by_rows(region, a, n), src.rearrange("(a p) n -> p a n", p=P))

        def load_split(landing, region, src):
            n = src.shape[1]
            landing.load(sp, region[:, 0:n], src[0:P, :])
            return landing.load(sp, region[0:CB_ROW, n:2 * n], src[P:C, :])

        class XA:
            pass

        L0 = XA()
        L0.dh, L0.hp, L0.mask, L0.scale = 16, 8, head16, 0.25
        L0.wq, L0.wk, L0.wkT = W[:, 0:512], W[:, 512:1024], W[:, 1024:1536]
        L0.wv = W[:, 1536:2048]
        L0.project_keys, L0.v_tiles, L0.split = True, 4, 4
        v_whole = v16[:, 544:544 + 1024].bitcast(F32).rearrange("p (t h c) -> p t h c", t=4, h=4)
        L0.inner = H * L0.dh
        L0.rows = W[0:1, 0:1024]
        L1 = XA()
        L1.dh, L1.hp, L1.mask, L1.scale = 64, 2, head64, 0.125
        L1.wq, L1.wk, L1.wkT = W[:, 0:2048], W[:, 2048:4096], W[:, 4096:6144]
        L1.wv, L1.wo = stage[:, 0:2048], stage[:, 2048:4096]
        L1.inner = H * L1.dh
        L1.project_keys, L1.v_tiles, L1.split = False, 2, 8
        L1.rows = stage[0:1, 0:1024]
        bk_scaled = small[:, 234:236]
        W1_OFF, W2_OFF = 2048, 3072
        CA_OFF = 4096
        cp = tail[:, 272:784].rearrange("p (a n) -> p a n", a=2)

        ctx_dram = d["ctx_768"][0].rearrange("(p t) c -> p (t c)", p=P)
        landed, halves = {}, {}
        turned = {}
        HI_BANK, B_BANK, LO_BANK = (0, 1), (2, 3), 4

        def load_chunk(c):
            if c >= 3:
                sp.wait(halves[c - 3])
            landed[c] = ld_ctx[c % 3].load(sp, ctx32[c % 3], ctx_dram[:, c * CW:(c + 1) * CW])

        x_in = ld_x.load(sp, x[:, :], d["x"][0])
        load_chunk(0)
        load_blocks(ld_w, L0.wq, d["L0_xattn_Wq"])
        l0_proj_in = load_split(ld_w, L0.wk, d["L0_xattn_Wk"])
        load_chunk(1)
        load_chunk(2)
        sp.wait(blank)
        CL, row = {}, 0
        for name, n in (("L0_xattn_bq", 2), ("L0_xattn_bk", 2), ("L0_xattn_bv", 2), ("L0_xattn_b1", 4),
                        ("L0_attn_c_attn_b", 4)):
            CL[name] = row
            biases_in = ld_bias.load(sp, col_in[row:row + n, :],
                                     d[name].rearrange("(r n) -> r n", n=P)[0:n, :])
            row += n
        CL["L0_ffn_b1"] = row
        nb1 = NE * F0 // P
        biases_in = ld_bias.load(sp, col_in[row:row + nb1, :],
                                 d["L0_ffn_b1"].rearrange("e (r n) -> (e r) n", n=P))

        def col(name, i):
            return cols[:, CL[name] + i:CL[name] + i + 1]

        pe.wait(constants, biases_in)
        tp(ps[:, 7, 0:P], col_in, ident[:, :])
        col_turned = pe.mark()
        act.wait(col_turned)
        copy(act, cols[:, :], ps[:, 7, 0:P])
        cols_ready = act.mark()
        pe.wait(cols_ready)
        dve.wait(cols_ready)

        def split_chunk(c):
            whole = ctx32[c % 3].rearrange("p (t c) -> p t c", t=CH)
            hi, lo = ctx16[c % 4][:, :, 0:C], ctx16[c % 4][:, :, C:2 * C]
            act.wait(landed[c])
            if c >= 4:
                act.wait(turned[c - 4])
            copy(act, hi, whole)
            hi_ready = act.mark()
            dve.wait(landed[c], hi_ready)
            tt(dve, lo, whole, hi, ALU.subtract)
            halves[c] = dve.mark()

        evac = {}

        def turn_chunk(c):
            c16 = ctx16[c % 4]
            banks = (HI_BANK[c % 2], B_BANK[c % 2], LO_BANK)
            hi, b, lo = (ps[:, n, :].bitcast(F16) for n in banks)
            pe.wait(halves[c], ident16_ready)
            if c >= 2:
                pe.wait(*evac[c - 2][0:2])
            for t in range(CH):
                s = slice(t * P, (t + 1) * P)
                tp(hi[:, s], c16[:, t, 0:P], ident16[:, :])
            hi_turned = pe.mark()
            for t in range(CH):
                s = slice(t * P, (t + 1) * P)
                tp(b[0:CB_ROW, s], c16[:, t, P:C], ident16[:, :])
                tp(b[CB_ROW:P, s], c16[:, t, C + P:2 * C], ident16[:, :])
            b_turned = pe.mark()
            if c >= 1:
                pe.wait(evac[c - 1][2])
            for t in range(CH):
                s = slice(t * P, (t + 1) * P)
                tp(lo[:, s], c16[:, t, C:C + P], ident16[:, :])
            turned[c] = lo_turned = pe.mark()
            s, w = slice(c * CH * P, (c + 1) * CH * P), CH * P
            act.wait(hi_turned)
            copy(act, ctxT_a_hi[:, s], hi[:, 0:w])
            hi_out = act.mark()
            dve.wait(b_turned)
            copy(dve, ctxT_b[:, s], b[:, 0:w])
            b_out = dve.mark()
            dve.wait(lo_turned)
            copy(dve, ctxT_a_lo[:, s], lo[:, 0:w])
            lo_out = dve.mark()
            dve.wait(b_out)
            copy(dve, ctxT_c[0:CB_ROW, s], ctxT_b[0:CB_ROW, s])
            evac[c] = (hi_out, b_out, lo_out, dve.mark())

        def split_weights(w, n, off, ready):
            top, rest = w[:, 0:n], w[0:CB_ROW, n:2 * n]
            cs = slice(off, off + n)
            pool.wait(*ready)
            ts(pool, top, top, VS, None, ALU.mult)
            pool.settle()
            copy(pool, wv16[:, 0, cs], top)
            pool.settle()
            tt(pool, wv16[:, 1, cs], top, wv16[:, 0, cs], ALU.subtract)
            pool.settle()
            ts(pool, rest, rest, VS, None, ALU.mult)
            pool.settle()
            copy(pool, wv16[0:CB_ROW, 2, cs], rest)
            pool.settle()
            tt(pool, wv16[0:CB_ROW, 3, cs], rest, wv16[0:CB_ROW, 2, cs], ALU.subtract)
            pool.settle()
            copy(pool, wv16[CB_ROW:P, 2, cs], rest)
            pool.settle()

        def split_wv(L, ready):
            split_weights(L.wv, L.inner, 0, (ready,))
            if L.project_keys:
                split_weights(L.wk, L.inner, L.inner, (L.folded,))
                ts(pool, bk_scaled, cols[:, CL["L0_xattn_bk"]:CL["L0_xattn_bk"] + 2], VS, None, ALU.mult)
                pool.settle()
            for b in range(L.v_tiles):
                v4 = v_tile(L, b)
                clear(pool, v4[:, :, L.dh:L.dh + 1], 1.0)
                clear(pool, v4[:, :, L.dh + 1:L.dh + 2], 0.0)
            if L.project_keys:
                clear(pool, v_whole, 0.0)
                pool.settle()
                clear(pool, v_whole[:, :, :, L.dh:L.dh + 1], 1.0)
            return pool.mark()

        def v_tile(L, b):
            w = L.split * (2 * L.dh + 2)
            return v16[:, b * w:(b + 1) * w].rearrange("p (h c) -> p h c", h=L.split)

        def fold_queries(L, wq_ready, bq, bk, get_xnT, banks, wk_banks):
            nI = L.inner // P
            hp = L.hp
            wq, wkT = by_rows(L.wq, 2, L.inner), by_rows(L.wkT, nI, 256)
            wkA, wkB = L.wk[:, 0:L.inner], L.wk[0:CB_ROW, L.inner:2 * L.inner]
            qT = p16[:, 0, 0:2 * P].bitcast(F32)
            spread = p16[:, 1:3, :].rearrange("p a b -> p (a b)").bitcast(F32)[:, 0:hp * P].rearrange(
                "p (h q) -> p h q", h=hp)
            qbank = banks[0][2]

            def by_head(ap):
                return ap.rearrange("p (h q) -> p h q", h=4)

            pe.wait(wq_ready, constants)
            if L is L0:
                pe.wait(get_xnT())
            wkT_out = []
            for i in range(0, nI, 2):
                bank = wk_banks[(i // 2) % len(wk_banks)]
                if i // 2 >= len(wk_banks):
                    pe.wait(wkT_out[-len(wk_banks)])
                for j in range(2):
                    tp(ps[:, bank, j * C:j * C + P], wkA[:, (i + j) * P:(i + j + 1) * P], ident[:, :])
                    tp(ps[:, bank, j * C + P:(j + 1) * C], wkB[:, (i + j) * P:(i + j + 1) * P],
                       ident[0:CB_ROW, 0:CB_ROW])
                turned = pe.mark()
                act.wait(turned)
                src = ps[:, bank, 0:2 * C].rearrange("p (j c) -> p j c", j=2)
                copy(act, wkT[:, i:i + 2, 0:C], src)
                copy(act, wkT[:, i:i + 2, C:256], src[:, :, P:C])
                wkT_out.append(act.mark())
                yield
            pe.wait(wkT_out[-1], get_xnT())
            folded, q_free, spread_free = [], None, None
            for i in range(nI):
                if q_free:
                    pe.wait(q_free)
                if bk and folded:
                    pe.wait(folded[-1])
                for a in range(2):
                    mm(ps[:, qbank, 0:P], wq[:, a, i * P:(i + 1) * P], xnT[:, a, :], a == 0, a == 1)
                q_ready = pe.mark()
                dve.wait(q_ready)
                if bq:
                    ts(dve, qT, ps[:, qbank, 0:P], col(bq, i), L.scale, ALU.add, ALU.mult)
                else:
                    ts(dve, qT, ps[:, qbank, 0:P], L.scale, None, ALU.mult)
                q_free = dve.settle()
                if spread_free:
                    dve.wait(spread_free)
                tt(dve, spread, bc(qT, 1, [P, hp, P]), bc(L.mask[:, :], 2, [P, hp, P]), ALU.mult)
                spread_ready = dve.mark()
                yield
                for j in range(0, hp, 4):
                    nh = min(4, hp)
                    w = nh * P
                    n = len(folded)
                    bank_a, bank_b, bank_c = banks[n % len(banks)]
                    pe.wait(spread_ready)
                    if n >= len(banks):
                        pe.wait(folded[n - len(banks)])
                    rhs = spread[:, j:j + nh, :]
                    mm(ps[:, bank_a, 0:w], wkT[:, i, 0:P], rhs, True, True)
                    mm(ps[:, bank_b, 0:w], wkT[:, i, P:256], rhs, True, True)
                    if bk:
                        mm(ps[0:1, bank_c, 0:w], col(bk, i), rhs, True, True)
                    got = pe.mark()
                    spread_free = got
                    s = slice((i * hp + j) * P, (i * hp + j + nh) * P)
                    act.wait(got)
                    copy(act, q_a_hi[:, s], ps[:, bank_a, 0:w])
                    if L.project_keys:
                        copy(act, q_m[0:CB_ROW, s], ps[0:CB_ROW, bank_b, 0:w])
                        hi_ready = act.mark()
                        rows = slice(16 * j, 16 * j + CB_ROW)
                        own = spread[rows, j:j + nh, :]
                        dve.wait(spread_ready)
                        for half in (slice(0, CB_ROW), slice(CB_ROW, P)):
                            copy(dve, by_head(q_s[half, s]), own)
                        dve.settle()
                        tt(dve, by_head(q_c[0:CB_ROW, s]), own, by_head(q_s[rows, s]), ALU.subtract)
                        dve.wait(hi_ready)
                    else:
                        copy(act, q_b[:, s], ps[:, bank_b, 0:w])
                        hi_ready = act.mark()
                        dve.wait(hi_ready)
                        tt(dve, q_a_lo[:, s], ps[:, bank_a, 0:w], q_a_hi[:, s], ALU.subtract)
                        tt(dve, q_c[0:CB_ROW, s], ps[0:CB_ROW, bank_b, 0:w], q_b[0:CB_ROW, s], ALU.subtract)
                        copy(dve, q_m[0:CB_ROW, s], q_b[0:CB_ROW, s])
                    if bk:
                        chi = att[0:1, 512 + n % 2 * 256:512 + (n % 2 + 1) * 256].bitcast(F16)
                        copy(dve, chi, ps[0:1, bank_c, 0:w])
                        dve.settle()
                        dve.wait(rows_blank)
                        copy(dve, q_m[HI_ROW:HI_ROW + 1, s], chi)
                        tt(dve, q_m[LO_ROW:LO_ROW + 1, s], ps[0:1, bank_c, 0:w], chi, ALU.subtract)
                    done = dve.mark()
                    folded.append(done)
                    yield
            pe.wait(*folded)
            L.folded = folded[-1]

        def attend(L, q_free=()):
            mpart = small[:, 64:64 + H * (len(DIRECT) + 1)].rearrange("p (h s) -> p h s", h=H)
            mx = small[:, 192:192 + H]
            BLK = MAXC * MAXB
            p16_flat = p16[:, :, :].rearrange("p a b -> p (a b)")
            copied = [p16_flat[:, n * BLK:(n + 1) * BLK] for n in range(4)]
            running = att[:, :].bitcast(F16)[:, 0:BLK]
            K_MAX = K_C if L.project_keys else CB_ROW
            left = [None] * 4
            taken = [L.folded] * 4
            total_copied = 0
            turn = 0
            def shift_columns(g):
                m = mx[:, 8 * g:8 * g + 8]
                reduce(m, mpart[:, 8 * g:8 * g + 8, :], AX.X, ALU.max).settle()
                ts(dve, m, m, -1.0, EXP_SHIFT, ALU.mult, ALU.add)
                return dve.mark()

            def shift_rows(g, k, bank, shift_ready):
                pe.wait(shift_ready)
                for j in range(4):
                    n = 8 * g + 4 * k + j
                    tp(ps[0:1, bank, j * P:(j + 1) * P], mx[:, n:n + 1], ident[:, :])
                turned = pe.mark()
                hi = L.rows[:, k * 256:(k + 1) * 256].bitcast(F16)
                s = slice(1024 * g + 512 * k, 1024 * g + 512 * (k + 1))
                dve.wait(turned, L.wv_ready)
                copy(dve, hi, ps[0:1, bank, :])
                dve.settle()
                tt(dve, q_c[LO_ROW:LO_ROW + 1, s], ps[0:1, bank, :], hi, ALU.subtract)
                copy(dve, q_c[HI_ROW:HI_ROW + 1, s], hi)
                return dve.mark()

            for h in range(H):
                hs = slice(h * P, (h + 1) * P)
                n_copied, n_direct = 0, 0
                for s in range(NMAX):
                    half = turn % 4
                    turn += 1
                    if left[half]:
                        pe.wait(left[half])
                    for b in range(MAXB):
                        k0 = (s * MAXB + b) * MAXC
                        o = ps[:, half * MAXB + b, 0:MAXC]
                        mm(o, q_a_hi[:, hs], ctxT_a_hi[:, k0:k0 + MAXC], True, False)
                        mm(o, q_m[0:K_MAX, hs], ctxT_c[0:K_MAX, k0:k0 + MAXC], False, True)
                    scored = pe.mark()
                    block = ps[:, half * MAXB:(half + 1) * MAXB, 0:MAXC]
                    if s in DIRECT:
                        dve.wait(scored)
                        reduce(mpart[:, h, n_direct:n_direct + 1], block, AX.XY, ALU.max)
                        n_direct += 1
                        left[half] = dve.mark()
                        continue
                    c = total_copied % 4
                    total_copied += 1
                    act.wait(scored, taken[c])
                    copy(act, copied[c].rearrange("p (a b) -> p a b", a=MAXB), block)
                    left[half] = copy_ready = act.mark()
                    n_copied += 1
                    if n_copied == 1:
                        before = c
                        continue
                    dve.wait(copy_ready)
                    if n_copied == 2:
                        tt(dve, running, copied[before], copied[c], ALU.max)
                    else:
                        tt(dve, running, running, copied[c], ALU.max)
                    taken[c] = dve.settle()
                    if n_copied == 2:
                        taken[before] = taken[c]
                w = BLK
                for _ in range(2):
                    w //= 2
                    tt(dve, running[:, 0:w], running[:, 0:w], running[:, w:2 * w], ALU.max)
                    dve.settle()
                reduce(mpart[:, h, n_direct:n_direct + 1], running[:, 0:w], AX.X, ALU.max).settle()
                if h == 7:
                    shift_ready = shift_columns(0)
                if h in (8, 9):
                    half = turn % 4
                    turn += 1
                    pe.wait(left[half])
                    left[half] = shift_rows(0, h - 8, MAXB * half, shift_ready)
                    rows_made = [left[half]]
            dh, vw = L.dh, 2 * L.dh + 2
            per_bank = 512 // vw if dh == 64 else 8
            V_BANK, O_BANK = 4, 5
            gw = 8 * dh

            def out_cols(h):
                o = (h % per_bank) * vw
                return ps[:, O_BANK + h // per_bank, o:o + vw]

            sc_free = {bank: left[bank // MAXB] for bank in range(8)}
            unit = 0
            v_free = None
            p_free = [None, None]
            pe.wait(L.wv_ready, left[V_BANK // MAXB], left[7 // MAXB])
            act.wait(*taken)
            S_BANKS = (0, 1, 2, 3) if L is L1 else (0, 1, 2, 3, 6)
            K_BANK = 7

            def p_split(part, b, j):
                o = (2 * part + b) * L.split * P + j * 512
                return p16_flat[:, o:o + 512]

            p_whole = [p16_flat[:, 2048 + 1024 * b:2048 + 1024 * (b + 1)].bitcast(F32) for b in range(2)]
            KW = 2 * P
            keys_read, keys_in, keys_left, values_in = {}, {}, None, {}
            score_scale = 1.0 / VS if L.project_keys else 1.0

            def project_keys(m):
                g, first = m // (NT // 2), m % (NT // 2) * KW
                ks = slice(first, first + KW)
                ws = slice(L.inner + g * P, L.inner + (g + 1) * P)
                b = m % 2
                if keys_left:
                    pe.wait(keys_left)
                products = ((wv16[:, 0, ws], ctxT_a_hi[:, ks]), (wv16[:, 1, ws], ctxT_a_hi[:, ks]),
                            (wv16[:, 0, ws], ctxT_a_lo[:, ks]), (wv16[:, 2, ws], ctxT_b[:, ks]),
                            (wv16[0:CB_ROW, 3, ws], ctxT_c[0:CB_ROW, ks]))
                for n, (wk, key) in enumerate(products):
                    mm(ps[:, K_BANK, 0:KW], wk, key, n == 0, n == len(products) - 1)
                projected = pe.mark()
                top, low = slice(0, CB_ROW), slice(CB_ROW, P)
                act.wait(projected)
                dve.wait(projected)
                if m >= 2:
                    act.wait(keys_read[m - 2])
                    dve.wait(keys_read[m - 2])
                    pool.wait(keys_read[m - 2])
                add_bias(k_both[top, b, 0, :], ps[top, K_BANK, 0:KW], bk_scaled[top, g:g + 1])
                hi0 = act.mark()
                ts(dve, k_both[low, b, 1, :], ps[low, K_BANK, 0:KW], bk_scaled[low, g:g + 1], None, ALU.add)
                hi1 = dve.mark()
                for j, (own, other, hi) in enumerate(((top, low, hi0), (low, top, hi1))):
                    dve.wait(hi)
                    low_part(k_both[other, b, j, :], ps[own, K_BANK, 0:KW], bk_scaled[own, g:g + 1],
                             k_both[own, b, j, :])
                left = dve.mark()
                for j, (own, hi) in enumerate(((top, hi0), (low, hi1))):
                    pool.wait(hi)
                    copy(pool, k_hi[top, b, j, :], k_both[own, b, j, :])
                    beside = pool.settle()
                keys_in[m] = (left, beside)
                return left

            def project_values(m, *free):
                g = m // (NT // 2)
                vs = slice(g * gw, (g + 1) * gw)
                if m:
                    pe.wait(values_in[m - 1])
                for u in range(2):
                    t = m % (NT // 2) * 2 + u
                    ks = slice(t * P, (t + 1) * P)
                    value_products(ps[:, V_BANK, u * gw:(u + 1) * gw], ks, vs)
                valued = pe.mark()
                w = 2 * 4 * vw
                v = v16[:, m % 2 * w:(m % 2 + 1) * w].rearrange("p (t h c) -> p t h c", t=2, h=4)
                vp = ps[:, V_BANK, 0:2 * gw].rearrange("p (t h c) -> p t h c", t=2, h=8)
                dve.wait(valued, *free)
                copy(dve, v[:, :, :, 0:dh], vp[:, :, 0:4, :])
                hi_ready = dve.mark()
                copy(dve, v_whole[:, m % 2 * 2:m % 2 * 2 + 2, :, 0:dh], vp[:, :, 4:8, :])
                dve.wait(hi_ready)
                tt(dve, v[:, :, :, dh + 2:vw], vp[:, :, 0:4, :], v[:, :, :, 0:dh], ALU.subtract)
                values_in[m] = dve.mark()

            def value_products(out, ks, vs):
                products = ((ctxT_a_hi[:, ks], wv16[:, 0, vs]), (ctxT_a_hi[:, ks], wv16[:, 1, vs]),
                            (ctxT_a_lo[:, ks], wv16[:, 0, vs]), (ctxT_b[:, ks], wv16[:, 2, vs]),
                            (ctxT_c[0:CB_ROW, ks], wv16[0:CB_ROW, 3, vs]))
                for n, (key, wv) in enumerate(products):
                    mm(out, key, wv, n == 0, n == len(products) - 1)

            if L.project_keys:
                keys_left = project_keys(0)
                project_values(0)
            att_ready = None
            for g in range(2):
                pending = None
                pe.wait(rows_made[g])
                for t in range(NT + 1):
                    if t < NT:
                        b = t % 2
                        ks = slice(t * P, (t + 1) * P)
                        vs = slice(g * gw, (g + 1) * gw)
                        m = (g * NT + t) // 2
                        if L.project_keys:
                            if t % 2 == 0 and m + 1 < NT:
                                keys_left = project_keys(m + 1)
                            v_free = values_in[m]
                        else:
                            if v_free:
                                pe.wait(v_free)
                            value_products(ps[:, V_BANK, 0:gw], ks, vs)
                            valued = pe.mark()
                        v4 = v_tile(L, (g * NT + t) % L.v_tiles)
                        vp = ps[:, V_BANK, 0:gw].rearrange("p (h c) -> p h c", h=8)
                        for j in range(2):
                            bank = S_BANKS[unit % len(S_BANKS)]
                            unit += 1
                            pe.wait(sc_free[bank])
                            if L.project_keys:
                                own = slice(t % 2 * P, (t % 2 + 1) * P)
                                score_terms = ((k_both[:, m % 2, j, own], q_s),
                                               (k_hi[0:K_C, m % 2, j, own], q_c))
                                pe.wait(*keys_in[m])
                            else:
                                score_terms = ((ctxT_a_hi[:, ks], q_a_hi), (ctxT_a_hi[:, ks], q_a_lo),
                                               (ctxT_a_lo[:, ks], q_a_hi), (ctxT_b[:, ks], q_b),
                                               (ctxT_c[0:K_C, ks], q_c))
                            for n, (key, q) in enumerate(score_terms):
                                rhs = q[0:key.shape[0], g * 1024 + j * 512:g * 1024 + (j + 1) * 512]
                                mm(ps[:, bank, :], key, rhs, n == 0, n == len(score_terms) - 1)
                            scored = pe.mark()
                            act.wait(scored)
                            if p_free[b]:
                                act.wait(p_free[b])
                            if L.project_keys and j == 1:
                                exp(p_whole[b], ps[:, bank, :], score_scale)
                                sc_free[bank] = exped = act.mark()
                                continue
                            phi, plo = p_split(0, b, j), p_split(1, b, j)
                            exp(phi, ps[:, bank, :], score_scale)
                            exp(ps[:, bank, :], ps[:, bank, :], score_scale)
                            exped = act.mark()
                            if j == 0 and not L.project_keys:
                                dve.wait(valued)
                                if p_free[b]:
                                    dve.wait(p_free[b])
                                copy(dve, v4[:, :, 0:dh], vp)
                                dve.settle()
                                tt(dve, v4[:, :, dh + 2:vw], vp, v4[:, :, 0:dh], ALU.subtract)
                                v_free = dve.mark()
                            dve.wait(exped)
                            tt(dve, plo, ps[:, bank, :], phi, ALU.subtract)
                            sc_free[bank] = low = dve.mark()
                    if L.project_keys and t < NT and t % 2:
                        keys_read[m] = scored
                    if g == 0 and t == 1:
                        shift_ready = shift_columns(1)
                    if g == 0 and t == 3:
                        for k in range(2):
                            bank = S_BANKS[unit % len(S_BANKS)]
                            unit += 1
                            pe.wait(sc_free[bank])
                            sc_free[bank] = shift_rows(1, k, bank, shift_ready)
                        rows_made.append(sc_free[bank])
                    if pending is not None:
                        pb, pready, pt = pending
                        pe.wait(*pready)
                        if pt == 0 and att_ready:
                            pe.wait(att_ready)
                        v4 = v_tile(L, (g * NT + pt) % L.v_tiles)
                        for h in range(L.split):
                            o = out_cols(h)
                            first = pt == 0 and h % per_bank == 0
                            kw = dict(skip_group_check=True)
                            hh = slice(h % 4 * P, (h % 4 + 1) * P)
                            hi, lo = (p_split(part, pb, h // 4)[:, hh] for part in range(2))
                            mm(o, hi, v4[:, h, :], first, False, **kw)
                            mm(o[:, 0:dh + 2], lo, v4[:, h, 0:dh + 2], False, pt == NT - 1, **kw)
                        for i in range(8 - L.split):
                            mm(ps[32 * i:32 * (i + 1), O_BANK, 256:256 + P], v_whole[:, (g * NT + pt) % 4, i, :],
                               p_whole[pb][:, i * P:(i + 1) * P], False, pt == NT - 1, **kw)
                        p_free[pb] = pe.mark()
                    if L.project_keys and t % 2 == 0 and t < NT and m + 1 < NT:
                        project_values(m + 1, *([p_free[1]] if p_free[1] else []))
                    pending = (b, (exped, v_free, low), t) if t < NT else None
                summed = p_free[(NT - 1) % 2]
                inv = small[:, 224:232]
                dve.wait(summed)
                for h0 in range(0, L.split, per_bank):
                    nh = min(per_bank, L.split - h0)
                    o = ps[:, O_BANK + h0 // per_bank, 0:nh * vw].rearrange("p (h c) -> p h c", h=nh)
                    a = att[:, g * gw + h0 * dh:g * gw + (h0 + nh) * dh].rearrange("p (h c) -> p h c", h=nh)
                    i = inv[:, h0:h0 + nh]
                    ts(dve, i, o[:, :, dh], VS, None, ALU.mult)
                    copy(dve, a, o[:, :, 0:dh])
                    dve.settle()
                    reciprocal(i, i)
                    tt(dve, a, o[:, :, dh + 2:vw], a, ALU.add)
                    dve.settle()
                    tt(dve, a, a, bc(i, 2, [P, nh, dh]), ALU.mult)
                if L.project_keys:
                    outT = att[:, 512:512 + P]
                    copy(dve, outT, ps[:, O_BANK, 256:256 + P])
                    pe.wait(dve.mark())
                    tp(ps[:, O_BANK, 384:384 + P], outT, ident[:, :])
                    dve.wait(pe.mark())
                    o = ps[:, O_BANK, 384:384 + P].rearrange("p (h c) -> p h c", h=4)
                    i = inv[:, 4:8]
                    ts(dve, i, o[:, :, dh], VS, None, ALU.mult)
                    dve.settle()
                    reciprocal(i, i).settle()
                    a = att[:, g * gw + 4 * dh:(g + 1) * gw].rearrange("p (h c) -> p h c", h=4)
                    tt(dve, a, o[:, :, 0:dh], bc(i, 2, [P, 4, dh]), ALU.mult)
                att_ready = dve.settle()
            return (att_ready,)

        split_chunk(0)
        split_chunk(1)
        xnT_ready = layernorm((x_in,), 5)
        steps = fold_queries(L0, l0_proj_in, "L0_xattn_bq", "L0_xattn_bk", lambda: xnT_ready, ((5, 6, 7),), (5,))
        for c in range(NCH):
            if c + 2 < NCH:
                split_chunk(c + 2)
            if c + 3 < NCH:
                load_chunk(c + 3)
            if c == 4:
                load_split(ld_w2, L0.wv, d["L0_xattn_Wv"])
                load_blocks(ld_w2, W[:, W1_OFF:], d["L0_xattn_W1"])
                load_blocks(ld_w2, W[:, W2_OFF:], d["L0_xattn_W2"])
                l0_rest_in = load_blocks(ld_w2, W[:, CA_OFF:], d["L0_attn_c_attn_w"])
            turn_chunk(c)
            next(steps, None)
        for _ in steps:
            pass
        L0.wv_ready = split_wv(L0, l0_rest_in)

        EXPERT0 = (stage[:, 0:4096], W[:, 5632:9728], W[:, 0:4096])

        def load_expert0(e, *free):
            region = EXPERT0[e % 3]
            sp.wait(*free)
            load_blocks(ld_exp[e % 3], region[:, 0:2048], d["L0_ffn_W1"][e])
            return load_blocks(ld_exp[e % 3], region[:, 2048:4096], d["L0_ffn_W2"][e])

        chunks_read = (halves[NCH - 1], turned[NCH - 1])
        sp.wait(*chunks_read)
        dve.wait(*chunks_read)
        clear(dve, bias_rows, 0.0)
        sp.wait(dve.settle())
        BR = {}
        for n, (name, lo_, w) in enumerate((("L0_xattn_b2", 0, D), ("L0_attn_c_attn_b", 2 * D, D),
                                            ("L0_attn_c_proj_b", 0, D), ("L1_xattn_bo", 0, D),
                                            ("L0_ffn_bg", 0, NE))):
            BR[name] = n
            ld_bias.load(sp, bias_rows[n:n + 1, 0:w],
                         d[name].rearrange("(a n) -> a n", a=1)[:, lo_:lo_ + w])
        load_blocks(ld_bias, tail[:, 272:784], d["L0_attn_c_proj_w"])
        load_blocks(ld_bias, tail[:, 256:272], d["L0_ffn_Wg"])
        tail_in = ld_bias.load(sp, bias2, d["L0_ffn_b2"])
        loaded = [load_expert0(0), load_expert0(1)]
        pe.wait(*evac[NCH - 2], *evac[NCH - 1])
        att_ready = attend(L0)

        attT = scratch[:, 0:2 * P].rearrange("p (a q) -> p a q", a=2)
        hT = scratch[:, 256:256 + 4 * P].rearrange("p (a q) -> p a q", a=4)
        pe.wait(*att_ready)
        pe.wait(tail_in)
        for i in range(2):
            tp(ps[:, 0, i * P:(i + 1) * P], att[:, i * P:(i + 1) * P], ident[:, :])
        turned = pe.mark()
        dve.wait(turned)
        for i in range(2):
            ts(dve, attT[:, i, :], ps[:, 0, i * P:(i + 1) * P], col("L0_xattn_bv", i), None, ALU.add)
        ready = dve.mark()
        pe.wait(ready)
        w1, w2 = wview(W1_OFF, 2, 512), wview(W2_OFF, 4, D)
        for f in range(4):
            for a in range(2):
                mm(ps[:, 1, f * P:(f + 1) * P], w1[:, a, f * P:(f + 1) * P], attT[:, a, :], a == 0, a == 1)
        ready = pe.mark()
        dve.wait(ready)
        for f in range(4):
            ts(dve, hT[:, f, :], ps[:, 1, f * P:(f + 1) * P], col("L0_xattn_b1", f), 0.0, ALU.add, ALU.max)
        ready = dve.mark()
        pe.wait(ready)
        for f in range(4):
            mm(ps[:, 2, 0:D], hT[:, f, :], w2[:, f, :], f == 0, False)
        mm(ps[:, 2, 0:D], row_select(BR["L0_xattn_b2"]), bias_rows, False, True)
        x_ready = residual(ps[:, 2, 0:D], pe.mark())
        loaded.append(load_expert0(2, x_ready))

        xnT_ready = layernorm(())
        ca = wview(CA_OFF, 2, 3 * D)
        qkT = scratch[:, 0:512].rearrange("p (a q) -> p a q", a=4)
        v_tok = scratch[:, 512:768]
        spread = scratch[:, 768:768 + 2048].rearrange("p (h q) -> p h q", h=H)
        probT = scratch[:, 768:768 + 2048].rearrange("p (h q) -> p h q", h=H)
        prob = scratch[:, 2816:2816 + 2048].rearrange("p (h q) -> p h q", h=H)
        pe.wait(xnT_ready)
        for n in range(4):
            for a in range(2):
                mm(ps[:, 1, n * P:(n + 1) * P], ca[:, a, n * P:(n + 1) * P], xnT[:, a, :], a == 0, a == 1)
        qk_in = pe.mark()
        for a in range(2):
            mm(ps[:, 2, 0:D], xnT[:, a, :], ca[:, a, 2 * D:3 * D], a == 0, False)
        mm(ps[:, 2, 0:D], row_select(BR["L0_attn_c_attn_b"]), bias_rows, False, True)
        v_in = pe.mark()
        dve.wait(qk_in)
        for n in range(4):
            ts(dve, qkT[:, n, :], ps[:, 1, n * P:(n + 1) * P], col("L0_attn_c_attn_b", n),
               0.25 if n < 2 else 1.0, ALU.add, ALU.mult)
        dve.settle()
        for i in range(2):
            tt(dve, spread[:, 8 * i:8 * i + 8, :], bc(qkT[:, i, :], 1, [P, 8, P]),
               bc(head16[:, :], 2, [P, 8, P]), ALU.mult)
        spread_ready = dve.mark()
        act.wait(v_in)
        copy(act, v_tok, ps[:, 2, 0:D])
        v_ready = act.mark()
        pe.wait(spread_ready)
        sc = ps[:, 4:8, :]
        for b in range(4):
            mm(ps[:, 4 + b, :], ident[:, :], bc(causal[:, :], 1, [P, 4, P]), True, False, skip_group_check=True)
            for j in range(4):
                h = 4 * b + j
                mm(ps[:, 4 + b, j * P:(j + 1) * P], spread[:, h, :], qkT[:, 2 + h // 8, :], False, True,
                   skip_group_check=True)
        scored = pe.mark()
        mx, tot = small[:, 16:32], small[:, 32:48]
        sch = sc.rearrange("p b (j q) -> p b j q", j=4)

        def by4(t):
            return t.rearrange("p (b j) -> p b j", b=4)

        dve.wait(scored)
        reduce(by4(mx), sch, AX.X, ALU.max).settle()
        tt(dve, prob.rearrange("p (b j) q -> p b j q", b=4), sch, bc(by4(mx), 3, [P, 4, 4, P]), ALU.subtract)
        centred = dve.mark()
        act.wait(centred)
        exp(prob, prob)
        exped = act.mark()
        dve.wait(exped)
        reduce(tot, prob, AX.X, ALU.add).settle()
        reciprocal(tot, tot).settle()
        pe.wait(exped)
        for h in range(H):
            tp(ps[:, h // 4, (h % 4) * P:(h % 4 + 1) * P], prob[:, h, :], ident[:, :])
        turned = pe.mark()
        act.wait(turned)
        copy(act, probT[:, 0:8, :].rearrange("p (b j) q -> p b (j q)", b=2), ps[:, 0:2, :])
        t1 = act.mark()
        dve.wait(turned)
        copy(dve, probT[:, 8:16, :].rearrange("p (b j) q -> p b (j q)", b=2), ps[:, 2:4, :])
        t2 = dve.mark()
        pe.wait(t1, t2, v_ready)
        for h in range(H):
            mm(ps[:, 4, h * 16:(h + 1) * 16], probT[:, h, :], v_tok[:, h * 16:(h + 1) * 16], True, True)
        ready = pe.mark()
        dve.wait(ready)
        tt(dve, att[:, 0:D].rearrange("p (h d) -> p h d", h=H), ps[:, 4, 0:D].rearrange("p (h d) -> p h d", h=H),
           bc(tot, 2, [P, H, 16]), ALU.mult)
        ready = dve.mark()
        attT_ready = transpose_act(att, 2, attT, (ready,), 5)
        pe.wait(attT_ready)
        for a in range(2):
            mm(ps[:, 6, 0:D], attT[:, a, :], cp[:, a, :], a == 0, False)
        mm(ps[:, 6, 0:D], row_select(BR["L0_attn_c_proj_b"]), bias_rows, False, True)
        x_ready = residual(ps[:, 6, 0:D], pe.mark())

        def gate(logits, ready, second_softmax):
            pr, w, mxe, tot = small[:, 240:248], small[:, 248:256], small[:, 256:257], small[:, 257:258]
            rank = small[:, 264:272]
            grid, eq = small[:, 272:336], small[:, 336:400]
            g3, q3 = (t.rearrange("p (e j) -> p e j", e=NE) for t in (grid, eq))
            dve.wait(ready)
            reduce(mxe, logits, AX.X, ALU.max).settle()
            ts(dve, pr, logits, mxe, None, ALU.subtract)
            t = dve.mark()
            act.wait(t)
            exp(pr, pr)
            t = act.mark()
            dve.wait(t)
            reduce(tot, pr, AX.X, ALU.add).settle()
            reciprocal(tot, tot).settle()
            ts(dve, pr, pr, tot, None, ALU.mult)
            dve.settle()
            pj, pe_ = bc(pr, 1, [P, NE, NE]), bc(pr, 2, [P, NE, NE])
            tt(dve, g3, pj, pe_, ALU.is_gt)
            tt(dve, q3, pj, pe_, ALU.is_equal)
            dve.settle()
            tt(dve, q3, q3, lower[:, :, :], ALU.mult)
            dve.settle()
            tt(dve, g3, g3, q3, ALU.add)
            dve.settle()
            reduce(rank, g3, AX.X, ALU.add).settle()
            ts(dve, rank, rank, 1.5, None, ALU.is_lt)
            if second_softmax:
                reduce(mxe, pr, AX.X, ALU.max).settle()
                ts(dve, pr, pr, mxe, None, ALU.subtract)
                t = dve.mark()
                act.wait(t)
                exp(pr, pr)
                t = act.mark()
                dve.wait(t)
            else:
                dve.settle()
            tt(dve, w, pr, rank, ALU.mult)
            dve.settle()
            reduce(tot, w, AX.X, ALU.add).settle()
            if not second_softmax:
                ts(dve, tot, tot, 1e-6, None, ALU.add)
                dve.settle()
            reciprocal(tot, tot).settle()
            ts(dve, w, w, tot, None, ALU.mult)
            return w, dve.settle()

        xnT_ready = layernorm(())
        pe.wait(xnT_ready)
        for a in range(2):
            mm(ps[:, 1, 0:NE], xnT[:, a, :], wg[:, a, :], a == 0, False)
        mm(ps[:, 1, 0:NE], row_select(BR["L0_ffn_bg"]), bias_rows[:, 0:NE], False, True)
        w_e, w_ready = gate(ps[:, 1, 0:NE], pe.mark(), False)
        wT = scratch[0:8, 4480:4480 + P]
        pe.wait(w_ready)
        tp(ps[0:8, 2, 0:P], w_e, ident[:, :])
        t = pe.mark()
        act.wait(t)
        copy(act, wT, ps[0:8, 2, 0:P])
        t = act.mark()
        pe.wait(t)
        mm(ps[:, 1, 0:D], wT, bias2, True, True)
        residual(ps[:, 1, 0:D], pe.mark())
        NF = F0 // P
        hT2 = [scratch[:, 2048 * 0 + 1024 * n:1024 * (n + 1)].rearrange("p (f q) -> p f q", f=NF) for n in range(2)]
        h_free, y_free, hidden = [None, None], [None, None], [None, None]

        def hidden0(e_):
            b = e_ % 2
            w1 = by_rows(EXPERT0[e_ % 3][:, 0:2048], 2, F0)
            pe.wait(loaded[e_])
            if hidden[b]:
                pe.wait(hidden[b])
            for k in range(NF // 4):
                bank = 2 + 2 * b + k
                for j in range(4):
                    f = 4 * k + j
                    for a in range(2):
                        mm(ps[:, bank, j * P:(j + 1) * P], w1[:, a, f * P:(f + 1) * P], xnT[:, a, :], a == 0, a == 1)
                summed = pe.mark()
                act.wait(summed)
                if h_free[b]:
                    act.wait(h_free[b])
                for j in range(4):
                    gelu(hT2[b][:, 4 * k + j, :], ps[:, bank, j * P:(j + 1) * P], col("L0_ffn_b1", e_ * NF + 4 * k + j))
            hidden[b] = act.mark()

        def down0(e_):
            b = e_ % 2
            w2 = by_rows(EXPERT0[e_ % 3][:, 2048:4096], NF, D)
            pe.wait(hidden[b])
            if y_free[b]:
                pe.wait(y_free[b])
            for f in range(NF):
                mm(ps[:, 6 + b, 0:D], hT2[b][:, f, :], w2[:, f, :], f == 0, f == NF - 1)
            y = pe.mark()
            h_free[b] = y
            dve.wait(y)
            weigh(ps[:, 6 + b, 0:D], w_e[:, e_:e_ + 1])
            y_free[b] = dve.settle()

        for e_ in range(NE + 1):
            if e_ < NE:
                hidden0(e_)
            else:
                steps = fold_queries(L1, l1_proj_in, None, None, lambda: xnT_ready,
                                     ((2, 3, 4), (5, 6, 7)), (0, 1))
                for _ in range(L1.inner // P // 2):
                    next(steps)
            if e_:
                down0(e_ - 1)
                done = h_free[(e_ - 1) % 2]
                if e_ + 2 < NE:
                    loaded.append(load_expert0(e_ + 2, done))
                elif e_ + 2 == NE:
                    sp.wait(done)
                    load_blocks(ld_w, L1.wq, d["L1_xattn_Wq"])
                    l1_proj_in = load_split(ld_w, L1.wk, d["L1_xattn_Wk"])
                elif e_ + 1 == NE:
                    sp.wait(done)
                    load_split(ld_w2, L1.wv, d["L1_xattn_Wv"])
                    l1_wv_in = load_blocks(ld_w2, L1.wo, d["L1_xattn_Wo"])
        x_ready = y_free[(NE - 1) % 2]

        xnT_ready = layernorm((), 2)
        clear(dve, q_c[CB_ROW:P, :].bitcast(F32), 0.0)
        act.wait(dve.settle())
        for _ in steps:
            pass
        L1.wv_ready = split_wv(L1, l1_wv_in)

        EXPERT1 = (W[:, 0:3072], W[:, 3072:6144], W[:, 6656:9728])
        wa, wr = by_rows(W[:, 6144:6656], 2, D), by_rows(W[:, 9728:], 2, NE)

        def load_expert1(e, *free):
            region = EXPERT1[e % 3]
            sp.wait(*free)
            load_blocks(ld_exp[e % 3], region[:, 0:1024], d["L1_ffn_kernel_gating_EDF"][e])
            load_blocks(ld_exp[e % 3], region[:, 1024:2048], d["L1_ffn_kernel_up_EDF"][e])
            return load_blocks(ld_exp[e % 3], region[:, 2048:3072], d["L1_ffn_kernel_down_EFD"][e])

        sp.wait(L1.folded)
        load_blocks(ld_bias, W[:, 6144:6656], d["L1_attn_W"])
        gate_in = load_blocks(ld_bias, W[:, 9728:], d["L1_ffn_router_kernel_DE"])
        loaded = [load_expert1(e, L1.folded) for e in range(3)]
        att_ready = attend(L1)
        attT = scratch[:, 0:1024].rearrange("p (a q) -> p a q", a=8)
        attT_ready = transpose_act(att, 8, attT, att_ready, 1)
        wo = by_rows(L1.wo, 8, D)
        pe.wait(attT_ready)
        for a in range(8):
            mm(ps[:, 3, 0:D], attT[:, a, :], wo[:, a, :], a == 0, False)
        mm(ps[:, 3, 0:D], row_select(BR["L1_xattn_bo"]), bias_rows, False, True)
        x_ready = residual(ps[:, 3, 0:D], pe.mark())

        NF1 = F1 // P

        xnT_ready = layernorm(())
        prob, mask = scratch[:, 0:128], scratch[:, 128:256]
        mx, tot, vac, spr = small[:, 16:17], small[:, 17:18], small[:, 18:19], small[:, 19:20]
        wsum = small[:, 20:22]
        pe.wait(xnT_ready)
        for a in range(2):
            mm(ps[:, 1, 0:P], xnT[:, a, :], xnT[:, a, :], a == 0, a == 1)
        scored = pe.mark()
        dve.wait(scored, x_ready)
        reduce(mx, ps[:, 1, 0:P], AX.X, ALU.max).settle()
        ts(dve, prob, ps[:, 1, 0:P], mx, 1.0 / 16, ALU.subtract, ALU.mult)
        t = dve.mark()
        act.wait(t)
        exp(prob, prob)
        t = act.mark()
        dve.wait(t)
        reduce(tot, prob, AX.X, ALU.add).settle()
        reciprocal(tot, tot).settle()
        ts(dve, prob, prob, tot, None, ALU.mult)
        dve.settle()
        ts(dve, mask, prob, 0.01, None, ALU.is_lt)
        dve.settle()
        tt(dve, mask, mask, prob, ALU.mult)
        dve.settle()
        reduce(vac, mask, AX.X, ALU.add)
        tt(dve, prob, prob, mask, ALU.subtract)
        dve.settle()
        reduce(spr, prob, AX.X, ALU.add).settle()
        ts(dve, spr, spr, 1e-9, None, ALU.add)
        dve.settle()
        reciprocal(spr, spr).settle()
        ts(dve, prob, prob, spr, None, ALU.mult)
        dve.wait(gate_in)
        reduce(wsum, wa, AX.X, ALU.add).settle()
        ts(dve, wsum, wsum, 0.01, None, ALU.mult)
        t = dve.mark()
        pe.wait(t)
        tp(ps[:, 2, 0:P], prob, ident[:, :])
        tp(ps[0:1, 2, P:2 * P], vac, ident[:, :])
        for a in range(2):
            tp(ps[0:1, 2, (2 + a) * P:(3 + a) * P], wsum[:, a:a + 1], ident[:, :])
        t = pe.mark()
        act.wait(t)
        probT = scratch[:, 256:384]
        rows = scratch[0:1, 384:384 + 384]
        copy(act, probT, ps[:, 2, 0:P])
        copy(act, rows, ps[0:1, 2, P:4 * P])
        t = act.mark()
        pe.wait(t)
        mm(ps[:, 3, 0:D], probT, xn[:, :], True, False)
        mm(ps[:, 3, 0:D], rows[:, 0:P], rows[:, P:3 * P], False, True)
        x_ready = residual(ps[:, 3, 0:D], pe.mark())

        xnT_ready = layernorm(())
        pe.wait(xnT_ready, gate_in)
        for a in range(2):
            mm(ps[:, 1, 0:NE], xnT[:, a, :], wr[:, a, :], a == 0, a == 1)
        w_e, _ = gate(ps[:, 1, 0:NE], pe.mark(), True)
        fuse = [scratch[:, 1024 * n:1024 * n + NF1 * P].rearrange("p (f q) -> p f q", f=NF1) for n in range(2)]
        sig = [scratch[:, 1024 * n + 512:1024 * n + 512 + NF1 * P] for n in range(2)]
        h_free, y_free, fused = [None, None], [None, None], [None, None]

        def hidden1(e_):
            b = e_ % 2
            region = EXPERT1[e_ % 3]
            wgt, wup = by_rows(region[:, 0:1024], 2, F1), by_rows(region[:, 1024:2048], 2, F1)
            gp, up = ps[:, 2 + 2 * b, :], ps[:, 3 + 2 * b, :]
            pe.wait(loaded[e_])
            if fused[b]:
                pe.wait(fused[b])
            made = []
            for o, w in ((gp, wgt), (up, wup)):
                for f in range(NF1):
                    for a in range(2):
                        mm(o[:, f * P:(f + 1) * P], w[:, a, f * P:(f + 1) * P], xnT[:, a, :], a == 0, a == 1)
                made.append(pe.mark())
            act.wait(made[0])
            if fused[b]:
                act.wait(fused[b])
            silu(sig[b], gp)
            dve.wait(act.mark())
            dve.wait(made[1])
            if h_free[b]:
                dve.wait(h_free[b])
            tt(dve, fuse[b].rearrange("p f q -> p (f q)"), up, sig[b], ALU.mult)
            fused[b] = dve.mark()

        def down1(e_):
            b = e_ % 2
            wdn = by_rows(EXPERT1[e_ % 3][:, 2048:3072], NF1, D)
            pe.wait(fused[b])
            if y_free[b]:
                pe.wait(y_free[b])
            for f in range(NF1):
                mm(ps[:, 6 + b, 0:D], fuse[b][:, f, :], wdn[:, f, :], f == 0, f == NF1 - 1)
            y = pe.mark()
            h_free[b] = y
            dve.wait(y)
            weigh(ps[:, 6 + b, 0:D], w_e[:, e_:e_ + 1])
            y_free[b] = dve.settle()

        for e_ in range(NE + 1):
            if e_ < NE:
                hidden1(e_)
            if e_:
                down1(e_ - 1)
                if e_ + 2 < NE:
                    loaded.append(load_expert1(e_ + 2, h_free[(e_ - 1) % 2]))
        sp.wait(y_free[(NE - 1) % 2])
        sp.wait(st_out.load(sp, out[0], x[:, :]))

        block = ctx.enter_context(nc.Block())
        block.tensor(pe.run)
        block.scalar(act.run)
        block.vector(dve.run)
        block.gpsimd(pool.run)
        block.sync(sp.run)


_OUTS = [((1, 128, 256), "float32")]


def kernel(**inputs):
    import numpy as _np
    import concourse.bacc as _bacc
    from concourse import mybir as _mybir
    from concourse.bass_utils import run_bass_kernel_spmd as _run

    nc = _bacc.Bacc("TRN2", target_bir_lowering=False, num_devices=1)
    arrays, args = {}, {}
    for name in inputs:
        a = _np.ascontiguousarray(inputs[name])
        arrays[f"in_{name}_dram"] = a
        args[name] = nc.dram_tensor(f"in_{name}_dram", a.shape, _mybir.dt.from_np(a.dtype), kind="ExternalInput").ap()
    shape, dtype = _OUTS[0]
    out = nc.dram_tensor("out_0_dram", shape, _mybir.dt.from_np(_np.dtype(dtype)), kind="ExternalOutput").ap()
    perceiver_kernel(nc, args, out)
    r = _run(nc, [arrays], core_ids=[0])
    return r.results[0]["out_0_dram"]
```
